# Optimizing a Trainium2 kernel written in Bass

```python
import numpy as np
import jax
import jax.numpy as jnp

def _softmax(x, axis=-1):
    return jax.nn.softmax(x, axis=axis)

def _gelu(x):
    return jax.nn.gelu(x, approximate=True)

def _silu(x):
    return jax.nn.silu(x)

def _sigmoid(x):
    return jax.nn.sigmoid(x)

def _layernorm(x, axis=-1, eps=1e-05):
    m = jnp.mean(x, axis=axis, keepdims=True)
    v = jnp.var(x, axis=axis, keepdims=True)
    return (x - m) / jnp.sqrt(v + eps)

def _scatter_add(tgt, idx, src, axis=0):
    return tgt.at[idx].add(src)

def _segment_sum(src, seg, n):
    return jax.ops.segment_sum(src, seg, n)
kernel_name = 'mk_prb_d1_jaxref_r4_10e0ce'

def setup_inputs(seed: int=0):
    np.random.seed(seed)
    _w = jnp.asarray

    def _L0_attn_setup():
        import jax, jax.numpy as jnp
        import numpy as np
        from jax import lax
        D_MODEL, D_INNER, D_STATE, D_CONV, DT_RANK = (256, 512, 16, 4, 64)
        B, L = (1, 512)

        def _reference_tuple_inner(x, W_in, conv_w, conv_b, W_x, W_dt, b_dt, A_log, D, W_out):
            b, l, dm = x.shape
            di, n = (A_log.shape[0], A_log.shape[1])
            x_and_res = x @ W_in
            xc, res = (x_and_res[..., :di], x_and_res[..., di:])
            k = conv_w.shape[1]
            xp = jnp.pad(xc, ((0, 0), (k - 1, 0), (0, 0)))
            xconv = conv_b
            for j in range(k):
                xconv = xconv + xp[:, j:j + l, :] * conv_w[:, j]
            xs = jax.nn.silu(xconv)
            x_dbl = xs @ W_x
            dt_r = x_dbl[..., :DT_RANK]
            Bm = x_dbl[..., DT_RANK:DT_RANK + n]
            Cm = x_dbl[..., DT_RANK + n:]
            dt = jax.nn.softplus(dt_r @ W_dt + b_dt)
            A = -jnp.exp(A_log)
            dA = jnp.exp(jnp.einsum('bld,dn->bldn', dt, A))
            dBx = jnp.einsum('bld,bln->bldn', dt, Bm) * xs[..., None]

            def step(h, inp):
                dA_t, dBx_t, C_t = inp
                h = dA_t * h + dBx_t
                y = jnp.einsum('bdn,bn->bd', h, C_t)
                return (h, y)
            h0 = jnp.zeros((b, di, n), x.dtype)
            hT, ys = lax.scan(step, h0, (dA.transpose(1, 0, 2, 3), dBx.transpose(1, 0, 2, 3), Cm.transpose(1, 0, 2)))
            y = ys.transpose(1, 0, 2) + xs * D
            y = y * jax.nn.silu(res)
            out = y @ W_out
            return (out, hT)
        key = jax.random.key(seed)
        ks = jax.random.split(key, 10)
        s = lambda d: 1.0 / np.sqrt(d)
        return {'x': jax.random.normal(ks[0], (B, L, D_MODEL), jnp.float32), 'W_in': jax.random.normal(ks[1], (D_MODEL, 2 * D_INNER), jnp.float32) * s(D_MODEL), 'conv_w': jax.random.normal(ks[2], (D_INNER, D_CONV), jnp.float32) * s(D_CONV), 'conv_b': jax.random.normal(ks[3], (D_INNER,), jnp.float32) * 0.01, 'W_x': jax.random.normal(ks[4], (D_INNER, DT_RANK + 2 * D_STATE), jnp.float32) * s(D_INNER), 'W_dt': jax.random.normal(ks[5], (DT_RANK, D_INNER), jnp.float32) * s(DT_RANK), 'b_dt': jax.random.normal(ks[6], (D_INNER,), jnp.float32) * 0.01, 'A_log': jnp.log(jnp.tile(jnp.arange(1.0, D_STATE + 1.0, dtype=jnp.float32), (D_INNER, 1))), 'D': jnp.ones((D_INNER,), jnp.float32), 'W_out': jax.random.normal(ks[7], (D_INNER, D_MODEL), jnp.float32) * s(D_INNER)}
    _L0_attn_in = _L0_attn_setup()

    def _L0_ffn_setup():
        import jax, jax.numpy as jnp
        import numpy as np
        B, S, H, NH, E, F = (4, 256, 256, 16, 8, 1024)
        D = H // NH
        EPS = 1e-05

        def _layernorm(x, g, b):
            mu = jnp.mean(x, axis=-1, keepdims=True)
            var = jnp.var(x, axis=-1, keepdims=True)
            return (x - mu) * jax.lax.rsqrt(var + EPS) * g + b
        key = jax.random.key(seed)
        ks = jax.random.split(key, 16)
        s = 0.02
        return {'x': jax.random.normal(ks[0], (B, S, H), jnp.float32), 'ln1_g': jnp.ones((H,), jnp.float32), 'ln1_b': jnp.zeros((H,), jnp.float32), 'ln2_g': jnp.ones((H,), jnp.float32), 'ln2_b': jnp.zeros((H,), jnp.float32), 'wq': jax.random.normal(ks[1], (H, H), jnp.float32) * s, 'bq': jnp.zeros((H,), jnp.float32), 'wk': jax.random.normal(ks[2], (H, H), jnp.float32) * s, 'bk': jnp.zeros((H,), jnp.float32), 'wv': jax.random.normal(ks[3], (H, H), jnp.float32) * s, 'bv': jnp.zeros((H,), jnp.float32), 'wo': jax.random.normal(ks[4], (H, H), jnp.float32) * s, 'bo': jnp.zeros((H,), jnp.float32), 'gate_w': jax.random.normal(ks[5], (H, E), jnp.float32) * s, 'gate_b': jnp.zeros((E,), jnp.float32), 'w1': jax.random.normal(ks[6], (E, H, F), jnp.float32) * s, 'b1': jnp.zeros((E, F), jnp.float32), 'w2': jax.random.normal(ks[7], (E, F, H), jnp.float32) * s, 'b2': jnp.zeros((E, H), jnp.float32)}
    _L0_ffn_in = _L0_ffn_setup()
    _d = {'L0_attn_x': _L0_attn_in['x'], 'L0_attn_W_in': _L0_attn_in['W_in'], 'L0_attn_conv_w': _L0_attn_in['conv_w'], 'L0_attn_conv_b': _L0_attn_in['conv_b'], 'L0_attn_W_x': _L0_attn_in['W_x'], 'L0_attn_W_dt': _L0_attn_in['W_dt'], 'L0_attn_b_dt': _L0_attn_in['b_dt'], 'L0_attn_A_log': _L0_attn_in['A_log'], 'L0_attn_D': _L0_attn_in['D'], 'L0_attn_W_out': _L0_attn_in['W_out'], 'L0_ffn_ln1_g': _L0_ffn_in['ln1_g'], 'L0_ffn_ln1_b': _L0_ffn_in['ln1_b'], 'L0_ffn_ln2_g': _L0_ffn_in['ln2_g'], 'L0_ffn_ln2_b': _L0_ffn_in['ln2_b'], 'L0_ffn_wq': _L0_ffn_in['wq'], 'L0_ffn_bq': _L0_ffn_in['bq'], 'L0_ffn_wk': _L0_ffn_in['wk'], 'L0_ffn_bk': _L0_ffn_in['bk'], 'L0_ffn_wv': _L0_ffn_in['wv'], 'L0_ffn_bv': _L0_ffn_in['bv'], 'L0_ffn_wo': _L0_ffn_in['wo'], 'L0_ffn_bo': _L0_ffn_in['bo'], 'L0_ffn_gate_w': _L0_ffn_in['gate_w'], 'L0_ffn_gate_b': _L0_ffn_in['gate_b'], 'L0_ffn_w1': _L0_ffn_in['w1'], 'L0_ffn_b1': _L0_ffn_in['b1'], 'L0_ffn_w2': _L0_ffn_in['w2'], 'L0_ffn_b2': _L0_ffn_in['b2']}
    _x0 = _d['L0_attn_x']
    _d['L0_attn_x'] = jax.random.normal(jax.random.fold_in(jax.random.key(seed), 1), (2, 2048, 256), dtype=_x0.dtype)
    del _x0
    return _d

def reference(L0_attn_x, L0_attn_W_in, L0_attn_conv_w, L0_attn_conv_b, L0_attn_W_x, L0_attn_W_dt, L0_attn_b_dt, L0_attn_A_log, L0_attn_D, L0_attn_W_out, L0_ffn_ln1_g, L0_ffn_ln1_b, L0_ffn_ln2_g, L0_ffn_ln2_b, L0_ffn_wq, L0_ffn_bq, L0_ffn_wk, L0_ffn_bk, L0_ffn_wv, L0_ffn_bv, L0_ffn_wo, L0_ffn_bo, L0_ffn_gate_w, L0_ffn_gate_b, L0_ffn_w1, L0_ffn_b1, L0_ffn_w2, L0_ffn_b2):

    def _L0_attn_ref(x, W_in, conv_w, conv_b, W_x, W_dt, b_dt, A_log, D, W_out):
        import jax, jax.numpy as jnp
        import numpy as np
        from jax import lax
        D_MODEL, D_INNER, D_STATE, D_CONV, DT_RANK = (256, 512, 16, 4, 64)
        B, L = (1, 512)

        def _reference_tuple_inner(x, W_in, conv_w, conv_b, W_x, W_dt, b_dt, A_log, D, W_out):
            b, l, dm = x.shape
            di, n = (A_log.shape[0], A_log.shape[1])
            x_and_res = x @ W_in
            xc, res = (x_and_res[..., :di], x_and_res[..., di:])
            k = conv_w.shape[1]
            xp = jnp.pad(xc, ((0, 0), (k - 1, 0), (0, 0)))
            xconv = conv_b
            for j in range(k):
                xconv = xconv + xp[:, j:j + l, :] * conv_w[:, j]
            xs = jax.nn.silu(xconv)
            x_dbl = xs @ W_x
            dt_r = x_dbl[..., :DT_RANK]
            Bm = x_dbl[..., DT_RANK:DT_RANK + n]
            Cm = x_dbl[..., DT_RANK + n:]
            dt = jax.nn.softplus(dt_r @ W_dt + b_dt)
            A = -jnp.exp(A_log)
            dA = jnp.exp(jnp.einsum('bld,dn->bldn', dt, A))
            dBx = jnp.einsum('bld,bln->bldn', dt, Bm) * xs[..., None]

            def step(h, inp):
                dA_t, dBx_t, C_t = inp
                h = dA_t * h + dBx_t
                y = jnp.einsum('bdn,bn->bd', h, C_t)
                return (h, y)
            h0 = jnp.zeros((b, di, n), x.dtype)
            hT, ys = lax.scan(step, h0, (dA.transpose(1, 0, 2, 3), dBx.transpose(1, 0, 2, 3), Cm.transpose(1, 0, 2)))
            y = ys.transpose(1, 0, 2) + xs * D
            y = y * jax.nn.silu(res)
            out = y @ W_out
            return (out, hT)
        return _reference_tuple_inner(x, W_in, conv_w, conv_b, W_x, W_dt, b_dt, A_log, D, W_out)[0]

    def _L0_ffn_ref(x, ln1_g, ln1_b, ln2_g, ln2_b, wq, bq, wk, bk, wv, bv, wo, bo, gate_w, gate_b, w1, b1, w2, b2):
        import jax, jax.numpy as jnp
        import numpy as np
        B, S, H, NH, E, F = (4, 256, 256, 16, 8, 1024)
        D = H // NH
        EPS = 1e-05

        def _layernorm(x, g, b):
            mu = jnp.mean(x, axis=-1, keepdims=True)
            var = jnp.var(x, axis=-1, keepdims=True)
            return (x - mu) * jax.lax.rsqrt(var + EPS) * g + b
        b, s, h = x.shape
        hn = _layernorm(x, ln1_g, ln1_b)
        q = (hn @ wq + bq).reshape(b, s, NH, D).transpose(0, 2, 1, 3)
        k = (hn @ wk + bk).reshape(b, s, NH, D).transpose(0, 2, 1, 3)
        v = (hn @ wv + bv).reshape(b, s, NH, D).transpose(0, 2, 1, 3)
        scores = jnp.einsum('bhqd,bhkd->bhqk', q, k) / jnp.sqrt(jnp.float32(D))
        attn = jax.nn.softmax(scores, axis=-1)
        o = jnp.einsum('bhqk,bhkd->bhqd', attn, v)
        o = o.transpose(0, 2, 1, 3).reshape(b, s, h)
        x = x + (o @ wo + bo)
        hn2 = _layernorm(x, ln2_g, ln2_b).reshape(-1, h)
        logits = hn2 @ gate_w + gate_b
        idx = jnp.argmax(logits, axis=-1)
        mid = jax.nn.relu(jnp.einsum('th,ehf->etf', hn2, w1) + b1[:, None, :])
        y = jnp.einsum('etf,efh->eth', mid, w2) + b2[:, None, :]
        moe = y[idx, jnp.arange(hn2.shape[0])]
        return x + moe.reshape(b, s, h)
    x = L0_attn_x
    xn = _layernorm(x, axis=-1)
    x = x + _L0_attn_ref(xn, L0_attn_W_in, L0_attn_conv_w, L0_attn_conv_b, L0_attn_W_x, L0_attn_W_dt, L0_attn_b_dt, L0_attn_A_log, L0_attn_D, L0_attn_W_out) + _L0_ffn_ref(xn, L0_ffn_ln1_g, L0_ffn_ln1_b, L0_ffn_ln2_g, L0_ffn_ln2_b, L0_ffn_wq, L0_ffn_bq, L0_ffn_wk, L0_ffn_bk, L0_ffn_wv, L0_ffn_bv, L0_ffn_wo, L0_ffn_bo, L0_ffn_gate_w, L0_ffn_gate_b, L0_ffn_w1, L0_ffn_b1, L0_ffn_w2, L0_ffn_b2)
    return x

_drawn_inputs = setup_inputs


def setup_inputs(seed=0):
    import zlib

    import numpy as np

    out = dict(_drawn_inputs(seed))
    spreads = {'L0_attn_D': (1.0, 0.2),
     'L0_ffn_ln1_g': (1.0, 0.6),
     'L0_ffn_ln1_b': (0.0, 0.636),
     'L0_ffn_ln2_g': (1.0, 0.2),
     'L0_ffn_ln2_b': (0.0, 0.1),
     'L0_ffn_bq': (0.0, 0.8),
     'L0_ffn_bk': (0.0, 2.0),
     'L0_ffn_bv': (0.0, 0.375),
     'L0_ffn_bo': (0.0, 0.1),
     'L0_ffn_gate_b': (0.0, 0.1),
     'L0_ffn_b1': (0.0, 0.383),
     'L0_ffn_b2': (0.0, 0.1)}
    factors = {'L0_attn_conv_b': 8.0,
     'L0_attn_b_dt': 38.471,
     'L0_ffn_wq': 8.0,
     'L0_ffn_wk': 8.0,
     'L0_ffn_wv': 5.045}
    for name, (base, spread) in spreads.items():
        noise = np.random.default_rng([zlib.crc32(name.encode()), seed]).standard_normal(out[name].shape)
        drawn = base * np.exp(spread * noise) if base else spread * noise
        out[name] = jnp.asarray(drawn.astype(out[name].dtype))
    for name, factor in factors.items():
        out[name] = (out[name] * factor).astype(out[name].dtype)
    return out
```

```python
from contextlib import ExitStack

import concourse.bass as bass
from concourse import mybir

ALU = mybir.AluOpType
ACT = mybir.ActivationFunctionType
AX = mybir.AxisListType
F32 = mybir.dt.float32
BF16 = mybir.dt.bfloat16
I32 = mybir.dt.int32
ds = bass.ds

P = 128
BANK = 512
EPS = 1e-5
HEADS = 16
HD = 16
GH = 4
VW = HD + 1
STACK = 6 * HD
Q_PARTS = [0, 0, 1, 0, 2, 1]
K_PARTS = [0, 1, 0, 2, 0, 1]
MT = 256


class Place:

    def __init__(self, nc, ctx, phase):
        self.nc, self.ctx, self.phase = nc, ctx, phase

    def sb(self, name, shape, dt=F32):
        return self.ctx.enter_context(self.nc.sbuf_tensor(f"{self.phase}_{name}", shape, dt))

    def ps(self, name, shape, dt=F32):
        return self.ctx.enter_context(self.nc.psum_tensor(f"{self.phase}_{name}", shape, dt))

    def sem(self, name):
        return self.ctx.enter_context(self.nc.semaphore(f"{self.phase}_{name}"))


class Chain:

    def __init__(self, eng, sem):
        self.eng, self.sem, self.base, self.n = eng, sem, 0, 0

    def at(self, base):
        self.base, self.n = base, 0

    def step(self, ins):
        self.n += 1
        ins.then_inc(self.sem, 1)
        self.eng.wait_ge(self.sem, self.base + self.n)

    def mark(self, ins):
        self.n += 1
        ins.then_inc(self.sem, 1)

    def join(self):
        self.eng.wait_ge(self.sem, self.base + self.n)


def bcast_rows(ap, n):
    return ap.rearrange("(o c) -> o c", o=1).to_broadcast([n, ap.shape[0]])


def make_identity(pool, ident, sem):
    pool.memset(ident[:, :], 0.0).then_inc(sem, 1)
    pool.wait_ge(sem, 1)
    pool.affine_select(out=ident[:, :], in_=ident[:, :], compare_op=ALU.not_equal, fill=1.0,
                       base=0, pattern=[[-1, P]], channel_multiplier=1).then_inc(sem, 1)


def rstd_steps(dve, chain, var, root, r, tmp, var_ready, root_ready, n):
    dve.tensor_scalar(var, var, EPS, None, ALU.add).then_inc(var_ready, 1)
    dve.wait_ge(root_ready, n)
    dve.wait_ge(var_ready, n)
    chain.step(dve.reciprocal(r, root))
    chain.step(dve.tensor_tensor(tmp, r, r, ALU.mult))
    chain.step(dve.tensor_tensor(tmp, tmp, var, ALU.mult))
    chain.step(dve.tensor_scalar(tmp, tmp, -0.5, 1.5, ALU.mult, ALU.add))
    chain.step(dve.tensor_tensor(r, r, tmp, ALU.mult))


def phase_norm(nc, x, g1, b1, xn_d, hn_d, slots_d):
    T, C = x.shape
    NT = T // P
    NG = T // BANK
    TG = NT // NG
    with ExitStack() as ctx:
        m = Place(nc, ctx, "norm")
        X = m.sb("x", [P, NT, C])
        HN = m.sb("hn", [P, NT, C])
        ST = m.sb("stats", [P, NT, 6])
        MV = m.sb("meanvar", [P, NT, 2])
        V = m.sb("var", [P, NT])
        ROOT = m.sb("root", [P, NT])
        R = m.sb("rstd", [P, NT])
        TMP = m.sb("tmp", [P, NT])
        G = m.sb("g", [P, C])
        B = m.sb("b", [P, C])
        Z = m.sb("zero", [P, 8, C])
        x_in = [m.sem(f"x_in{g}") for g in range(NG)]
        gb_in = m.sem("gb_in")
        stats = m.sem("stats")
        chain_s = m.sem("chain")
        var_ready = m.sem("var_ready")
        root_ready = m.sem("root_ready")
        xn_done = m.sem("xn_done")
        hn_raw = m.sem("hn_raw")
        hn_mul = m.sem("hn_mul")
        hn_done = m.sem("hn_done")
        zeroed = m.sem("zeroed")
        stored = m.sem("stored")
        zero_stored = m.sem("zero_stored")
        rows = slots_d.shape[0]

        with nc.Block() as block:

            @block.sync
            def _(sp):
                for g in range(NG):
                    sp.dma_start(X[:, g * TG:(g + 1) * TG, :],
                                 x[g * BANK:(g + 1) * BANK, :].rearrange("(t p) c -> p t c", p=P)
                                 ).then_inc(x_in[g], 16)
                sp.dma_start(G[:, :], bcast_rows(g1, P)).then_inc(gb_in, 16)
                sp.dma_start(B[:, :], bcast_rows(b1, P)).then_inc(gb_in, 16)
                sp.wait_ge(zeroed, 1)
                n = 0
                for r in range(0, rows, 8 * P):
                    k = min(8, (rows - r) // P)
                    sp.dma_start(slots_d[r:r + k * P, :].rearrange("(t p) c -> p t c", p=P),
                                 Z[:, 0:k, :]).then_inc(zero_stored, 16)
                    n += 1
                for g in range(NG):
                    sp.wait_ge(xn_done, (g + 1) * TG)
                    sp.dma_start(xn_d[g * BANK:(g + 1) * BANK, :].rearrange("(t p) c -> p t c", p=P),
                                 X[:, g * TG:(g + 1) * TG, :]).then_inc(stored, 16)
                for g in range(NG):
                    sp.wait_ge(hn_done, g + 1)
                    sp.dma_start(hn_d[g * BANK:(g + 1) * BANK, :].rearrange("(t p) c -> p t c", p=P),
                                 HN[:, g * TG:(g + 1) * TG, :]).then_inc(stored, 16)
                sp.wait_ge(zero_stored, 16 * n)
                sp.wait_ge(stored, 32 * NG)

            @block.vector
            def _(dve):
                chain = Chain(dve, chain_s)
                dve.memset(Z[:, :, :], 0.0).then_inc(zeroed, 1)
                for rnd in range(2):
                    for g in range(NG):
                        if rnd == 0:
                            dve.wait_ge(x_in[g], 16)
                        with dve.Fori(g * TG, (g + 1) * TG) as t:
                            if rnd == 1:
                                dve.wait_ge(xn_done, t + 1)
                            dve.bn_stats(ST[:, ds(t, 1), :], X[:, ds(t, 1), :]).then_inc(stats, 1)
                    dve.wait_ge(stats, (2 * rnd + 1) * NT)
                    for t in range(NT):
                        dve.bn_aggr(MV[:, t, :], ST[:, t, :]).then_inc(stats, 1)
                    dve.wait_ge(stats, (2 * rnd + 2) * NT)
                    chain.step(dve.tensor_copy(V[:, :], MV[:, :, 1]))
                    rstd_steps(dve, chain, V[:, :], ROOT[:, :], R[:, :], TMP[:, :],
                               var_ready, root_ready, rnd + 1)
                    with dve.Fori(0, NT) as t:
                        out = X if rnd == 0 else HN
                        dve.tensor_scalar(out[:, ds(t, 1), :], X[:, ds(t, 1), :], MV[:, ds(t, 1), 0:1],
                                          R[:, ds(t, 1)], ALU.subtract, ALU.mult
                                          ).then_inc(xn_done if rnd == 0 else hn_raw, 1)

            @block.scalar
            def _(act):
                for n in range(2):
                    act.wait_ge(var_ready, n + 1)
                    act.activation(ROOT[:, :], V[:, :], ACT.Sqrt).then_inc(root_ready, 1)

            @block.gpsimd
            def _(pool):
                pool.wait_ge(gb_in, 32)
                for g in range(NG):
                    h = HN[:, g * TG:(g + 1) * TG, :]
                    pool.wait_ge(hn_raw, (g + 1) * TG)
                    pool.tensor_tensor(h, h, G[:, :].unsqueeze(1).to_broadcast([P, TG, C]), ALU.mult
                                       ).then_inc(hn_mul, 1)
                    pool.wait_ge(hn_mul, g + 1)
                    pool.tensor_tensor(h, h, B[:, :].unsqueeze(1).to_broadcast([P, TG, C]), ALU.add
                                       ).then_inc(hn_done, 1)


def phase_project(nc, xn_d, hn_d, wq, bq, wk, bk, wv, bv, xnT_d, parts_d, v_d, batches):
    T, C = xn_d.shape
    KC = C // P
    TG = BANK // P
    NB = T // batches // BANK
    GB = HEADS // GH
    assert NB % 2 == 0
    with ExitStack() as ctx:
        m = Place(nc, ctx, "proj")
        IN = [[m.sb(f"in{s}{n}", [P, TG, C]) for n in range(2)] for s in range(2)]
        TR = [[m.sb(f"tr{s}{n}", [P, KC, BANK]) for n in range(2)] for s in range(2)]
        WQK = m.sb("wqk", [P, 2, KC, C])
        WV = m.sb("wv", [P, KC, C])
        BQK = m.sb("bqk", [P, 2, KC])
        BV = m.sb("bv", [1, C])
        ONE = m.sb("one", [1, P])
        ident = m.sb("ident", [P, P])
        QF = [m.sb(f"qf{n}", [P, BANK]) for n in range(2)]
        QR = [m.sb(f"qr{n}", [P, BANK]) for n in range(2)]
        QP = [m.sb(f"qp{n}", [P, 3, BANK], BF16) for n in range(2)]
        VS = [m.sb(f"vs{n}", [P, HEADS, VW]) for n in range(2)]
        pT = [m.ps(f"pT{n}", [P, BANK]) for n in range(4)]
        pQ = [m.ps(f"pQ{n}", [P, BANK]) for n in range(2)]
        pV = [m.ps(f"pV{n}", [P, BANK]) for n in range(2)]
        w_in = m.sem("w_in")
        id_ready = m.sem("id_ready")
        ones_ready = m.sem("ones_ready")
        rows_in = [m.sem(f"rows_in{s}") for s in range(2)]
        rows_used = [m.sem(f"rows_used{s}") for s in range(2)]
        turned = [m.sem(f"turned{n}") for n in range(2)]
        turned_sb = [m.sem(f"turned_sb{n}") for n in range(2)]
        xnT_out = [m.sem(f"xnT_out{s}") for s in range(2)]
        qk_ps = m.sem("qk_ps")
        qk_f = m.sem("qk_f")
        qk_hi = m.sem("qk_hi")
        qk_r = m.sem("qk_r")
        qk_mid = m.sem("qk_mid")
        qk_low = m.sem("qk_low")
        parts_out = [m.sem(f"parts_out{n}") for n in range(2)]
        v_ps = m.sem("v_ps")
        v_sb = m.sem("v_sb")
        v_out = [m.sem(f"v_out{n}") for n in range(2)]

        def chunks(eng, body):
            with eng.Fori(0, batches) as b:
                with eng.Fori(0, NB // 2) as i:
                    for s in range(2):
                        body(b * NB + i * 2 + s, b * (NB // 2) + i, s, b, i * 2 + s)

        with nc.Block() as block:

            @block.gpsimd
            def _(pool):
                make_identity(pool, ident, id_ready)

                def body(c, u, s, b, cb):
                    pool.wait_ge(rows_used[s], u + 1)
                    for n, src in enumerate((xn_d, hn_d)):
                        pool.dma_start(IN[s][n][:, :, :],
                                       src[ds(c * BANK, BANK), :].rearrange("(t p) c -> p t c", p=P)
                                       ).then_inc(rows_in[s], 16)
                chunks(pool, body)

            @block.sync
            def _(sp):
                for n, w in enumerate((wq, wk)):
                    sp.dma_start(WQK[:, n, :, :], w.rearrange("(k p) n -> p k n", p=P)).then_inc(w_in, 16)
                for n, w in enumerate((bq, bk)):
                    sp.dma_start(BQK[:, n, :], w).then_inc(w_in, 16)
                sp.dma_start(WV[:, :, :], wv.rearrange("(k p) n -> p k n", p=P)).then_inc(w_in, 16)
                sp.dma_start(BV[:, :], bv.rearrange("(o n) -> o n", o=1)).then_inc(w_in, 16)

                def body(c, u, s, b, cb):
                    sp.wait_ge(turned_sb[0], c * KC + 2 * KC)
                    sp.dma_start(xnT_d[:, ds(c * BANK, BANK)].rearrange("(k p) t -> p k t", p=P),
                                 TR[s][0][:, :, :]).then_inc(xnT_out[s], 16)
                    for r in range(4):
                        qk, k = divmod(r, KC)
                        sp.wait_ge(qk_low, c * 4 + (r + 1))
                        sp.dma_start(parts_d[qk][:, ds(b * C + k * P, P), ds(cb * BANK, BANK)]
                                     .rearrange("a r t -> r a t"), QP[r % 2][:, :, :]
                                     ).then_inc(parts_out[r % 2], 16)
                    for t in range(TG):
                        sp.wait_ge(v_sb, c * TG + (t + 3))
                        sp.dma_start(v_d[ds(b * GB, GB), ds(cb * BANK + t * P, P), :]
                                     .rearrange("g t x -> t g x"), VS[t % 2][:, :, :]
                                     ).then_inc(v_out[t % 2], 16)
                chunks(sp, body)
                n = batches * NB
                for s in range(2):
                    sp.wait_ge(xnT_out[s], 16 * (n // 2 + 1))
                    sp.wait_ge(parts_out[s], 16 * (2 * n + 1))
                    sp.wait_ge(v_out[s], 16 * (2 * n + 1))

            @block.tensor
            def _(pe):
                for s in range(2):
                    pe.sem_inc(rows_used[s], 1)
                pe.wait_ge(w_in, 16 * 6)
                pe.wait_ge(id_ready, 2)
                pe.wait_ge(ones_ready, 3)

                def body(c, u, s, b, cb):
                    pe.wait_ge(rows_in[s], u * 32 + 32)
                    for n in range(2):
                        for k in range(KC):
                            pe.wait_ge(turned_sb[n], c * KC + (k + 1))
                            for t in range(TG):
                                mm = pe.transpose(pT[2 * n + k][:, t * P:(t + 1) * P],
                                                  IN[s][n][:, t, k * P:(k + 1) * P], ident[:, :])
                            mm.then_inc(turned[n], 1)
                    pe.wait_ge(turned_sb[1], c * KC + 2 * KC)
                    pe.sem_inc(rows_used[s], 1)
                    for r in range(4):
                        qk, k = divmod(r, KC)
                        pe.wait_ge(qk_hi, c * 4 + (r + 1))
                        for kk in range(KC):
                            mm = pe.matmul(pQ[r % 2][:, :], WQK[:, qk, kk, k * P:(k + 1) * P],
                                           TR[s][1][:, kk, :], start=(kk == 0), stop=(kk == KC - 1))
                        mm.then_inc(qk_ps, 1)
                    for t in range(TG):
                        pe.wait_ge(v_sb, c * TG + (t + 1))
                        for kk in range(KC):
                            pe.matmul(pV[t % 2][:, 0:C], TR[s][1][:, kk, t * P:(t + 1) * P],
                                      WV[:, kk, :], start=(kk == 0), stop=False)
                        pe.matmul(pV[t % 2][:, 0:C], ONE[:, :], BV[:, :], start=False, stop=True
                                  ).then_inc(v_ps, 1)
                chunks(pe, body)

            @block.scalar
            def _(act):
                act.sem_inc(turned_sb[0], KC)
                act.sem_inc(qk_hi, 2)
                act.sem_inc(v_sb, 2)
                for s in range(2):
                    act.sem_inc(xnT_out[s], 16)
                    act.sem_inc(parts_out[s], 16)
                    act.sem_inc(v_out[s], 16)
                act.wait_ge(w_in, 16 * 6)
                act.wait_ge(ones_ready, 3)

                def body(c, u, s, b, cb):
                    act.wait_ge(xnT_out[s], u * 16 + 16)
                    for k in range(KC):
                        act.wait_ge(turned[0], c * KC + (k + 1))
                        act.copy(TR[s][0][:, k, :], pT[k][:, :]).then_inc(turned_sb[0], 1)
                    for r in range(4):
                        qk, k = divmod(r, KC)
                        act.wait_ge(qk_ps, c * 4 + (r + 1))
                        act.wait_ge(qk_r, c * 4 + (r + 1))
                        act.activation(QF[r % 2][:, :], pQ[r % 2][:, :], ACT.Identity,
                                       bias=BQK[:, qk, k:k + 1]).then_inc(qk_f, 1)
                        act.wait_ge(parts_out[r % 2], c * 32 + (16 * (r // 2) + 16))
                        act.activation(QP[r % 2][:, 0, :], pQ[r % 2][:, :], ACT.Identity,
                                       bias=BQK[:, qk, k:k + 1]).then_inc(qk_hi, 1)
                    for t in range(TG):
                        act.wait_ge(v_ps, c * TG + (t + 1))
                        act.wait_ge(v_out[t % 2], c * 32 + (16 * (t // 2) + 16))
                        act.copy(VS[t % 2][:, :, 0:HD],
                                 pV[t % 2][:, 0:C].rearrange("p (h d) -> p h d", d=HD)).then_inc(v_sb, 1)
                chunks(act, body)

            @block.vector
            def _(dve):
                dve.sem_inc(turned_sb[1], KC)
                dve.sem_inc(qk_r, 2)
                dve.memset(ONE[:, :], 1.0).then_inc(ones_ready, 1)
                for n in range(2):
                    dve.memset(VS[n][:, :, HD:VW], 1.0).then_inc(ones_ready, 1)

                def body(c, u, s, b, cb):
                    for k in range(KC):
                        dve.wait_ge(turned[1], c * KC + (k + 1))
                        dve.tensor_copy(TR[s][1][:, k, :], pT[2 + k][:, :]).then_inc(turned_sb[1], 1)
                    for r in range(4):
                        n = r % 2
                        dve.wait_ge(qk_f, c * 4 + (r + 1))
                        dve.wait_ge(qk_hi, c * 4 + (r + 3))
                        dve.tensor_tensor(QR[n][:, :], QF[n][:, :], QP[n][:, 0, :], ALU.subtract
                                          ).then_inc(qk_r, 1)
                        dve.wait_ge(qk_r, c * 4 + (r + 3))
                        dve.tensor_copy(QP[n][:, 1, :], QR[n][:, :]).then_inc(qk_mid, 1)
                        dve.wait_ge(qk_mid, c * 4 + (r + 1))
                        dve.tensor_tensor(QP[n][:, 2, :], QR[n][:, :], QP[n][:, 1, :], ALU.subtract
                                          ).then_inc(qk_low, 1)
                chunks(dve, body)


def phase_attention(nc, parts_d, v_d, oraw_d, batches):
    L = parts_d.shape[3]
    QC = L // BANK
    KT = L // P
    QT = BANK // P
    GC = GH * HD
    NG = batches * HEADS // GH
    NI = NG * QC
    RING = 4
    NSM = GH * QT * QC
    SM_KT = NSM // KT
    STACK_M = STACK + 3
    LOADS = 13
    assert RING % QC == 0 and NI % RING == 0 and SM_KT * KT == NSM
    with ExitStack() as ctx:
        m = Place(nc, ctx, "attn")
        KS = [m.sb(f"ks{s}", [P, GH, L], BF16) for s in range(RING)]
        QS = [m.sb(f"qs{s}", [P, GH, BANK], BF16) for s in range(RING)]
        VS = [m.sb(f"vs{s}", [P, KT, GH, VW]) for s in range(RING)]
        PR = [m.sb(f"pr{n}", [P, 2, BANK]) for n in range(4)]
        OE = [m.sb(f"oe{n}", [P, BANK]) for n in range(2)]
        MX = m.sb("mx", [P, NSM])
        MN = m.sb("mn", [P, GH * QT])
        MR = m.sb("mr", [P, GH * QT])
        MS = m.sb("ms", [P, P // (GH * QT), GH * QT], BF16)
        MB = [m.sb(f"mb{n}", [P, P], BF16) for n in range(2)]
        ident = m.sb("ident", [P, P])
        identb = m.sb("identb", [P, P], BF16)
        pS = [m.ps(f"pS{n}", [P, 2, BANK]) for n in range(2)]
        pX = [m.ps(f"pX{n}", [P, BANK]) for n in range(2)]
        pO = m.ps("pO", [P, BANK])
        pM = m.ps("pM", [P, P], BF16)
        ops_in = [m.sem(f"ops_in{s}") for s in range(RING)]
        mrow_in = [m.sem(f"mrow_in{s}") for s in range(RING)]
        id_ready = m.sem("id_ready")
        ones_ready = m.sem("ones_ready")
        rest_zero = m.sem("rest_zero")
        x_ps = m.sem("x_ps")
        x_max = m.sem("x_max")
        mchain_s = m.sem("mchain")
        m_split = m.sem("m_split")
        m_ps = m.sem("m_ps")
        m_sb = m.sem("m_sb")
        s_ps = m.sem("s_ps")
        p_sb = m.sem("p_sb")
        pv_done = m.sem("pv_done")
        o_sb = m.sem("o_sb")
        o_out = [m.sem(f"o_out{n}") for n in range(2)]

        def where(i, s):
            i = i + s // RING if s >= RING else i
            s = s % RING
            return i * (RING // QC) + s // QC, s % QC, s, i

        def bodies(eng, body):
            if NI > RING:
                with eng.Fori(0, NI // RING - 1) as i:
                    for s in range(RING):
                        body(i, s, 9)
            for s in range(RING):
                body(NI // RING - 1, s, RING - 1 - s)

        with nc.Block() as block:

            @block.sync
            def _(sp):
                def load(i, s):
                    g, qc, slot, _ = where(i, s)
                    for a in range(6):
                        rows = slice(a * HD, (a + 1) * HD)
                        sp.dma_start(QS[slot][rows, :, :],
                                     parts_d[0, Q_PARTS[a]][ds(g * GC, GC), qc * BANK:(qc + 1) * BANK]
                                     .rearrange("(h c) t -> c h t", c=HD)).then_inc(ops_in[slot], 16)
                        sp.dma_start(KS[slot][rows, :, :],
                                     parts_d[1, K_PARTS[a]][ds(g * GC, GC), :]
                                     .rearrange("(h c) t -> c h t", c=HD)).then_inc(ops_in[slot], 16)
                    sp.dma_start(VS[slot][:, :, :, :],
                                 v_d[ds(g, 1), :, :].rearrange("g (k p) x -> p (g k) x", p=P)
                                 ).then_inc(ops_in[slot], 16)

                def max_rows(i, s):
                    _, _, slot, _ = where(i, s)
                    sp.wait_ge(m_sb, i * RING + (s + 1))
                    for a in range(3):
                        sp.dma_start(QS[slot][STACK + a:STACK + a + 1, :, :],
                                     MB[s % 2][a * GH * QT:(a + 1) * GH * QT, :]
                                     ).then_inc(mrow_in[slot], 16)

                for n in range(2):
                    sp.sem_inc(o_out[n], 16)
                for s in range(3):
                    load(0, s)
                max_rows(0, 0)

                def body(i, s, left):
                    if left >= 3:
                        sp.wait_ge(pv_done, i * (RING * KT) + (s * KT + 2))
                        load(i, s + 3)
                    if left >= 1:
                        max_rows(i, s + 1)
                    sp.wait_ge(o_sb, i * RING + (s + 2))
                    sp.dma_start(oraw_d[ds(i * RING + s, 1), :, :].rearrange("i p q -> p (i q)"),
                                 OE[s % 2][:, :]).then_inc(o_out[s % 2], 16)
                bodies(sp, body)
                for n in range(2):
                    sp.wait_ge(o_out[n], 16 * (NI // 2 + 1))

            @block.gpsimd
            def _(pool):
                make_identity(pool, ident, id_ready)
                pool.wait_ge(id_ready, 2)
                for s in range(RING):
                    pool.memset(KS[s][STACK:STACK_M, :, :], 1.0).then_inc(ones_ready, 1)
                    pool.wait_ge(ones_ready, s + 1)

            @block.tensor
            def _(pe):
                def scores_max(i, s, n0, n1):
                    _, _, slot, use = where(i, s)
                    for n in range(n0, n1):
                        head, rest = divmod(n, QT * QC)
                        qt, part = divmod(rest, QC)
                        if n == 0:
                            pe.wait_ge(ops_in[slot], use * (16 * LOADS) + 16 * LOADS)
                        pe.wait_ge(x_max, i * (RING * NSM) + (s * NSM + n + 1))
                        pe.matmul(pX[n % 2][:, :], QS[slot][0:STACK, head, qt * P:(qt + 1) * P],
                                  KS[slot][0:STACK, head, part * BANK:(part + 1) * BANK],
                                  start=True, stop=True).then_inc(x_ps, 1)

                def max_turn(i, s):
                    pe.wait_ge(m_split, i * RING + (s + 1))
                    pe.transpose(pM[:, :], MS[:, :, :], identb[:, :]).then_inc(m_ps, 1)

                def scores(i, s, kt, pair):
                    _, _, slot, use = where(i, s)
                    if kt == 0 and pair == 0:
                        pe.wait_ge(mrow_in[slot], use * 48 + 48)
                    z = s * 2 * KT + kt * 2 + pair
                    pe.wait_ge(p_sb, i * (RING * 2 * KT) + (z + 1))
                    for h in range(2):
                        mm = pe.matmul(pS[pair][:, h, :],
                                       KS[slot][0:STACK_M, 2 * pair + h, kt * P:(kt + 1) * P],
                                       QS[slot][0:STACK_M, 2 * pair + h, :], start=True, stop=True)
                    mm.then_inc(s_ps, 1)

                def values(i, s, kt):
                    if kt == 0:
                        pe.wait_ge(o_sb, i * RING + (s + 1))
                    pe.wait_ge(p_sb, i * (RING * 2 * KT) + (s * 2 * KT + kt * 2 + 4))
                    for h in range(GH):
                        mm = pe.matmul(pO[32 * h:32 * h + VW, :], VS[s][:, kt, h, :],
                                       PR[2 * (kt % 2) + h // 2][:, h % 2, :],
                                       start=(kt == 0), stop=(kt == KT - 1))
                    mm.then_inc(pv_done, 1)

                pe.sem_inc(pv_done, 2)
                pe.wait_ge(id_ready, 3)
                scores_max(0, 0, 0, NSM)
                pe.wait_ge(rest_zero, 1)
                max_turn(0, 0)
                scores_max(0, 1, 0, NSM)
                pe.wait_ge(ones_ready, RING)
                scores(0, 0, 0, 0)
                scores(0, 0, 0, 1)

                def body(i, s, left):
                    for kt in range(KT):
                        n = kt * SM_KT
                        ahead = [(i, s, kt + 1)] if kt + 1 < KT else [(i, s + 1, 0)] if left >= 1 else []
                        if ahead:
                            scores(*ahead[0], 0)
                        if left >= 2:
                            scores_max(i, s + 2, n, n + SM_KT // 4)
                        if ahead:
                            scores(*ahead[0], 1)
                        if left >= 2:
                            scores_max(i, s + 2, n + SM_KT // 4, n + SM_KT // 2)
                        values(i, s, kt)
                        if left >= 2:
                            scores_max(i, s + 2, n + SM_KT // 2, n + SM_KT)
                        if kt == 1 and left >= 1:
                            max_turn(i, s + 1)
                bodies(pe, body)

            @block.scalar
            def _(act):
                act.sem_inc(p_sb, 2)

                def body(i, s, left):
                    for kt in range(KT):
                        act.wait_ge(pv_done, i * (RING * KT) + (s * KT + kt + 1))
                        for pair in range(2):
                            act.wait_ge(s_ps, i * (RING * 2 * KT) + (s * 2 * KT + kt * 2 + pair + 1))
                            act.activation(PR[2 * (kt % 2) + pair][:, :, :], pS[pair][:, :, :], ACT.Exp,
                                           scale=HD ** -0.5).then_inc(p_sb, 1)
                    act.wait_ge(o_out[s % 2], i * (16 * RING // 2) + (16 * (s // 2) + 16))
                    act.wait_ge(pv_done, i * (RING * KT) + ((s + 1) * KT + 2))
                    act.copy(OE[s % 2][:, :], pO[:, :]).then_inc(o_sb, 1)
                bodies(act, body)

            @block.vector
            def _(dve):
                chain = Chain(dve, mchain_s)
                dve.memset(pO[:, :], 0.0).then_inc(o_sb, 1)
                dve.wait_ge(id_ready, 2)
                dve.tensor_copy(identb[:, :], ident[:, :]).then_inc(id_ready, 1)
                dve.memset(MS[:, 3:, :], 0.0).then_inc(rest_zero, 1)
                dve.sem_inc(x_max, 2)

                def maxima(i, s, n0, n1):
                    for n in range(n0, n1):
                        dve.wait_ge(x_ps, i * (RING * NSM) + (s * NSM + n + 1))
                        dve.tensor_reduce(MX[:, n:n + 1], pX[n % 2][:, :], AX.X, ALU.max
                                          ).then_inc(x_max, 1)

                def split(i, s):
                    chain.at(i * (RING * 4) + s * 4)
                    dve.wait_ge(x_max, i * (RING * NSM) + ((s + 1) * NSM + 2))
                    chain.step(dve.tensor_reduce(MN[:, :], MX[:, :].rearrange("p (x a) -> p x a", a=QC),
                                                 AX.X, ALU.max, negate=True))
                    chain.step(dve.tensor_copy(MS[:, 0, :], MN[:, :]))
                    chain.step(dve.tensor_tensor(MR[:, :], MN[:, :], MS[:, 0, :], ALU.subtract))
                    chain.step(dve.tensor_copy(MS[:, 1, :], MR[:, :]))
                    dve.tensor_tensor(MS[:, 2, :], MR[:, :], MS[:, 1, :], ALU.subtract).then_inc(m_split, 1)

                def turned(i, s):
                    dve.wait_ge(m_ps, i * RING + (s + 1))
                    dve.tensor_copy(MB[s % 2][:, :], pM[:, :]).then_inc(m_sb, 1)

                maxima(0, 0, 0, NSM)
                split(0, 0)
                turned(0, 0)
                maxima(0, 1, 0, NSM)

                def body(i, s, left):
                    if left >= 1:
                        split(i, s + 1)
                    if left >= 2:
                        maxima(i, s + 2, 0, 2 * SM_KT)
                    if left >= 1:
                        turned(i, s + 1)
                    if left >= 2:
                        maxima(i, s + 2, 2 * SM_KT, NSM)
                bodies(dve, body)


def phase_mamba(nc, xnT_d, w_in, conv_w, conv_b, w_x, w_dt, b_dt, a_log, d_skip, w_out, bc_d, mo_d, batches):
    C, T = xnT_d.shape
    DI = w_out.shape[0]
    N = a_log.shape[1] // (DI // P)
    R = w_dt.shape[0]
    KC, JT = C // P, DI // P
    NCH = T // BANK
    CB = NCH // batches
    QN = 4
    NQ = N // QN
    TG = BANK // P
    TAPS = conv_w.shape[1] // JT
    NPS = 2 * JT + 1 + JT
    assert NCH % 2 == 0 and CB % 2 == 0 and NQ == 4 and JT == 4
    with ExitStack() as ctx:
        m = Place(nc, ctx, "mamba")
        WIN = m.sb("win", [P, KC, 2 * DI])
        WX = m.sb("wx", [P, JT, R + 2 * N])
        WDT = m.sb("wdt", [R, DI])
        WOUT = m.sb("wout", [P, JT, C])
        CW = m.sb("cw", [P, JT, TAPS])
        CBI = m.sb("cb", [P, JT])
        BDT = m.sb("bdt", [P, JT])
        AN = m.sb("an", [P, JT, N])
        DS = m.sb("ds", [P, JT])
        MK = m.sb("mk", [P, NCH])
        ident = m.sb("ident", [P, P])
        HS = m.sb("hs", [P, JT, N])
        CR = m.sb("cr", [P, JT, TAPS - 1])
        XT = [m.sb(f"xt{s}", [P, KC, BANK]) for s in range(2)]
        XC = m.sb("xc", [P, JT, BANK + TAPS - 1])
        XV = m.sb("xv", [P, JT, BANK])
        XS = [m.sb(f"xs{s}", [P, JT, BANK]) for s in range(2)]
        GT = [m.sb(f"gt{s}", [P, JT, BANK]) for s in range(2)]
        DT = [m.sb(f"dt{s}", [P, JT, BANK]) for s in range(2)]
        U = [m.sb(f"u{s}", [P, JT, BANK]) for s in range(2)]
        DR = m.sb("dr", [R + 2 * N, BANK])
        BQ = [m.sb(f"bq{n}", [P, 2, QN, BANK]) for n in range(2)]
        DA = [m.sb(f"da{n}", [P, QN, BANK]) for n in range(2)]
        DB = [m.sb(f"db{n}", [P, QN, BANK]) for n in range(2)]
        H = [m.sb(f"h{n}", [P, QN, BANK]) for n in range(2)]
        Z = m.sb("z", [P, JT, BANK])
        MO = m.sb("mo", [P, TG, C])
        E = XC[:, :, TAPS - 1:TAPS - 1 + BANK]
        pY = [m.ps(f"pY{j}", [P, BANK]) for j in range(JT)]
        pP = [m.ps(f"pP{n}", [P, BANK]) for n in range(2)]
        pW = [m.ps(f"pW{n}", [P, BANK]) for n in range(2)]
        w_ld = m.sem("w_ld")
        id_ready = m.sem("id_ready")
        ready = m.sem("ready")
        a_ready = m.sem("a_ready")
        xt_in = [m.sem(f"xt_in{s}") for s in range(2)]
        p_ps = m.sem("p_ps")
        p_sb = m.sem("p_sb")
        steps_s = m.sem("steps")
        conv_done = m.sem("conv_done")
        cr_kept = m.sem("cr_kept")
        xc_free = m.sem("xc_free")
        xs_done = m.sem("xs_done")
        bc_out = m.sem("bc_out")
        bc_there = m.sem("bc_there")
        b_in = [m.sem(f"b_in{n}") for n in range(2)]
        c_in = [m.sem(f"c_in{n}") for n in range(2)]
        e_done = m.sem("e_done")
        dt_done = m.sem("dt_done")
        u_done = m.sem("u_done")
        da_done = m.sem("da_done")
        db_done = m.sem("db_done")
        scanned = m.sem("scanned")
        hs_kept = m.sem("hs_kept")
        hc_done = m.sem("hc_done")
        y_done = m.sem("y_done")
        z_raw = m.sem("z_raw")
        z_done = m.sem("z_done")
        w_ps = m.sem("w_ps")
        w_sb = m.sem("w_sb")
        mo_out = m.sem("mo_out")
        UNITS = NQ * JT

        def bodies(eng, body):
            body(0, 0, 0, True, NCH == 1, NCH > 2)
            looped = max(0, (NCH - 3) // 2)
            if looped:
                with eng.Fori(0, looped) as i:
                    body(i * 2 + 1, i, 1, False, False, True)
                    body(i * 2 + 2, i + 1, 0, False, False, True)
            for c in range(1 + 2 * looped, NCH):
                body(c, c // 2, c % 2, False, c == NCH - 1, c + 2 < NCH)

        with nc.Block() as block:

            @block.sync
            def _(sp):
                for dst, src in ((WIN[:, :, :], w_in.rearrange("(k p) n -> p k n", p=P)),
                                 (WX[:, :, :], w_x.rearrange("(k p) n -> p k n", p=P)),
                                 (WDT[:, :], w_dt),
                                 (WOUT[:, :, :], w_out.rearrange("(k p) n -> p k n", p=P)),
                                 (CW[:, :, :], conv_w.rearrange("p (j k) -> p j k", j=JT)),
                                 (CBI[:, :], conv_b), (BDT[:, :], b_dt),
                                 (AN[:, :, :], a_log.rearrange("p (j n) -> p j n", j=JT)), (DS[:, :], d_skip)):
                    sp.dma_start(dst, src).then_inc(w_ld, 16)

                def load_x(c, s):
                    sp.dma_start(XT[s][:, :, :],
                                 xnT_d[:, ds(c * BANK, BANK)].rearrange("(k p) t -> p k t", p=P)
                                 ).then_inc(xt_in[s], 16)

                def load_rows(c, q, n, done):
                    rows = bc_d[ds(c, 1), n * N + q * QN:n * N + (q + 1) * QN, :]
                    sp.dma_start(BQ[q % 2][:, n, :, :],
                                 rows.rearrange("c n t -> c (n t)").to_broadcast([P, QN * BANK])
                                 ).then_inc(done[q % 2], 16)

                def load_b(c, q):
                    if q == 0:
                        sp.wait_ge(bc_out, c * 16 + 16)
                        sp.sem_inc(bc_there, 1)
                    sp.wait_ge(db_done, c * UNITS + (q * JT + JT))
                    load_rows(c, q, 0, b_in)

                def load_c(c, q):
                    sp.wait_ge(hc_done, c * UNITS + (q * JT + JT))
                    load_rows(c, q, 1, c_in)

                def store_mo(c):
                    sp.wait_ge(w_sb, c * 2 + 4)
                    sp.dma_start(mo_d[ds(c * BANK, BANK), :].rearrange("(t p) c -> p t c", p=P),
                                 MO[:, :, :]).then_inc(mo_out, 16)

                def store_bc(c):
                    sp.wait_ge(p_sb, c * NPS + (2 * JT + 3))
                    sp.dma_start(bc_d[ds(c, 1), :, :].rearrange("c n t -> (c n) t"), DR[R:R + 2 * N, :]
                                 ).then_inc(bc_out, 16)

                load_x(0, 0)
                load_x(1, 1)
                store_bc(0)
                load_b(0, 0)
                load_c(0, 0)
                load_b(0, 1)

                def body(c, u, s, first, last, more):
                    if more:
                        sp.wait_ge(p_ps, c * NPS + 2 * JT)
                        load_x(c + 2, s)
                    load_c(c, 1)
                    load_b(c, 2)
                    load_c(c, 2)
                    if not first:
                        store_mo(c - 1)
                    load_b(c, 3)
                    load_c(c, 3)
                    if not last:
                        store_bc(c + 1)
                        load_b(c + 1, 0)
                        load_c(c + 1, 0)
                        load_b(c + 1, 1)
                    else:
                        store_mo(c)
                bodies(sp, body)
                sp.wait_ge(mo_out, 16 * NCH + 16)

            @block.gpsimd
            def _(pool):
                pool.sem_inc(db_done, 8)
                make_identity(pool, ident, id_ready)

                def u_step(c, s):
                    pool.wait_ge(dt_done, c + 1)
                    pool.tensor_tensor(U[s][:, :, :], DT[s][:, :, :], XS[s][:, :, :], ALU.mult
                                       ).then_inc(u_done, 1)
                    pool.wait_ge(u_done, c + 1)

                u_step(0, 0)

                def body(c, u, s, first, last, more):
                    for k in range(UNITS):
                        q, j = divmod(k, JT)
                        if j == 0:
                            pool.wait_ge(b_in[q % 2], c * 32 + (16 * (q // 2) + 16))
                        pool.wait_ge(scanned, c * UNITS + (k + 1))
                        pool.tensor_tensor(DB[k % 2][:, :, :], BQ[q % 2][:, 0, :, :],
                                           U[s][:, j, :].unsqueeze(1).to_broadcast([P, QN, BANK]), ALU.mult
                                           ).then_inc(db_done, 1)
                        if k == 14 and not last:
                            u_step(c + 1, 1 - s)
                bodies(pool, body)

            @block.scalar
            def _(act):
                act.wait_ge(w_ld, 16 * 9)
                act.activation(AN[:, :, :], AN[:, :, :], ACT.Exp).then_inc(a_ready, 1)

                def bank(s, n):
                    return pP[(s + n) % 2]

                def conv_in(c, s):
                    act.wait_ge(xc_free, c + 1)
                    for j in range(JT):
                        act.wait_ge(p_ps, c * NPS + (j + 1))
                        act.copy(XC[:, j, TAPS - 1:], bank(s, j)[:, :]).then_inc(p_sb, 1)

                def conv_out(c, s):
                    for j in range(JT):
                        act.wait_ge(conv_done, c * JT + (j + 1))
                        act.activation(XS[s][:, j, :], XV[:, j, :], ACT.Silu).then_inc(xs_done, 1)
                    for j in range(JT):
                        n = JT + j
                        act.wait_ge(p_ps, c * NPS + (n + 1))
                        act.activation(GT[s][:, j, :], bank(s, n)[:, :], ACT.Silu).then_inc(p_sb, 1)

                def low_rank(c, s, first=False):
                    act.wait_ge(p_ps, c * NPS + (2 * JT + 1))
                    if not first:
                        act.wait_ge(bc_out, c * 16)
                    act.copy(DR[:, :], bank(s, 2 * JT)[0:R + 2 * N, :]).then_inc(p_sb, 1)

                def soft_in(c, s):
                    for j in range(JT):
                        n = 2 * JT + 1 + j
                        act.wait_ge(p_ps, c * NPS + (n + 1))
                        act.activation(XV[:, j, :], bank(s, n)[:, :], ACT.Identity, bias=BDT[:, j:j + 1]
                                       ).then_inc(p_sb, 1)
                    act.wait_ge(p_sb, c * NPS + (NPS + 2))
                    act.wait_ge(cr_kept, c + 1)
                    act.activation(E, XV[:, :, :], ACT.Abs).then_inc(e_done, 1)
                    act.wait_ge(e_done, c * 3 + 1)
                    act.activation(E, E, ACT.Exp, scale=-1.0).then_inc(e_done, 1)
                    act.wait_ge(e_done, c * 3 + 2)
                    act.activation(DT[s][:, :, :], E, ACT.Ln, bias=1.0).then_inc(e_done, 1)

                def decay(c, s, k):
                    q, j = divmod(k, JT)
                    act.wait_ge(scanned, c * UNITS + (k + 1))
                    for n in range(QN):
                        ins = act.activation(DA[k % 2][:, n, :], DT[s][:, j, :], ACT.Exp,
                                             scale=AN[:, j, q * QN + n:q * QN + n + 1])
                    ins.then_inc(da_done, 1)

                def mo_copy(c):
                    act.wait_ge(mo_out, c * 16 + 16)
                    for n in range(2):
                        act.wait_ge(w_ps, c * 2 + (n + 3))
                        act.copy(MO[:, 2 * n:2 * n + 2, :], pW[n][:, :]).then_inc(w_sb, 1)

                act.sem_inc(p_sb, 2)
                act.sem_inc(w_sb, 2)
                act.sem_inc(mo_out, 16)
                act.wait_ge(ready, 1)
                conv_in(0, 0)
                conv_out(0, 0)
                low_rank(0, 0, first=True)
                soft_in(0, 0)

                def body(c, u, s, first, last, more):
                    act.wait_ge(dt_done, c + 1)
                    for k in range(UNITS):
                        decay(c, s, k)
                        if k == 4 and not first:
                            mo_copy(c - 1)
                        if not last:
                            if k == 1:
                                conv_in(c + 1, 1 - s)
                            if k == 5:
                                conv_out(c + 1, 1 - s)
                            if k == 8:
                                low_rank(c + 1, 1 - s)
                            if k == 11:
                                soft_in(c + 1, 1 - s)
                    if last:
                        mo_copy(c)
                bodies(act, body)

            @block.tensor
            def _(pe):
                def into(c, s, n, pairs, rows=P):
                    pe.wait_ge(p_sb, c * NPS + (n + 1))
                    for i, (w, x) in enumerate(pairs):
                        mm = pe.matmul(pP[(s + n) % 2][0:rows, :], w, x, start=(i == 0),
                                       stop=(i == len(pairs) - 1))
                    mm.then_inc(p_ps, 1)

                def project_in(c, u, s, half):
                    pe.wait_ge(xt_in[s], u * 16 + 16)
                    for j in range(JT):
                        n = half * JT + j
                        into(c, s, n, [(WIN[:, k, n * P:(n + 1) * P], XT[s][:, k, :]) for k in range(KC)])

                def low_rank(c, s):
                    pe.wait_ge(xs_done, c * JT + JT)
                    into(c, s, 2 * JT, [(WX[:, j, :], XS[s][:, j, :]) for j in range(JT)], R + 2 * N)

                def dt_in(c, s):
                    pe.wait_ge(p_sb, c * NPS + (2 * JT + 3))
                    for j in range(JT):
                        into(c, s, 2 * JT + 1 + j, [(WDT[:, j * P:(j + 1) * P], DR[0:R, :])])

                def project_out(c):
                    pe.wait_ge(z_done, c * JT + JT)
                    for n in range(2):
                        pe.wait_ge(w_sb, c * 2 + (n + 1))
                        for t in range(2):
                            for j in range(JT):
                                mm = pe.matmul(pW[n][:, t * C:(t + 1) * C],
                                               Z[:, j, (2 * n + t) * P:(2 * n + t + 1) * P],
                                               WOUT[:, j, :], start=(j == 0), stop=(j == JT - 1))
                        mm.then_inc(w_ps, 1)

                pe.sem_inc(y_done, 2)
                pe.sem_inc(w_ps, 2)
                pe.wait_ge(w_ld, 16 * 9)
                pe.wait_ge(id_ready, 2)
                project_in(0, 0, 0, 0)
                project_in(0, 0, 0, 1)
                low_rank(0, 0)
                dt_in(0, 0)

                def body(c, u, s, first, last, more):
                    if not last:
                        project_in(c + 1, u + s, 1 - s, 0)
                    for k in range(UNITS):
                        q, j = divmod(k, JT)
                        if q == 0:
                            pe.wait_ge(z_raw, c * JT + (j + 1))
                        pe.wait_ge(hc_done, c * UNITS + (k + 9))
                        for n in range(QN):
                            mm = pe.matmul(pY[j][:, :], ident[:, :], H[k % 2][:, n, :],
                                           start=(q == 0 and n == 0), stop=(q == NQ - 1 and n == QN - 1))
                        mm.then_inc(y_done, 1)
                        if k == 1 and not first:
                            project_out(c - 1)
                        if not last:
                            if k == 3:
                                project_in(c + 1, u + s, 1 - s, 1)
                            if k == 6:
                                low_rank(c + 1, 1 - s)
                            if k == 8:
                                dt_in(c + 1, 1 - s)
                    if last:
                        project_out(c)
                bodies(pe, body)

            @block.vector
            def _(dve):
                def conv(c, s, chain):
                    dve.wait_ge(p_sb, c * NPS + (JT + 2))
                    chain.step(dve.tensor_scalar(XC[:, :, 0:TAPS - 1], CR[:, :, :], MK[:, ds(c, 1)],
                                                 None, ALU.mult))
                    for k in range(TAPS):
                        for j in range(JT):
                            x = XC[:, j, k:k + BANK]
                            if k == 0:
                                ins = dve.tensor_scalar(XV[:, j, :], x, CW[:, j, k:k + 1], CBI[:, j:j + 1],
                                                        ALU.mult, ALU.add)
                            else:
                                ins = dve.scalar_tensor_tensor(out=XV[:, j, :], in0=x, scalar=CW[:, j, k:k + 1],
                                                               in1=XV[:, j, :], op0=ALU.mult, op1=ALU.add)
                            if k == TAPS - 1:
                                ins.then_inc(conv_done, 1)
                        if k < TAPS - 1:
                            chain.step(ins)
                    dve.wait_ge(conv_done, c * JT + JT)
                    dve.tensor_copy(CR[:, :, :], XC[:, :, BANK:BANK + TAPS - 1]).then_inc(cr_kept, 1)
                    dve.wait_ge(cr_kept, c + 1)

                def softplus(c, s, chain):
                    dve.wait_ge(e_done, c * 3 + 3)
                    chain.step(dve.tensor_scalar(U[s][:, :, :], E, 1.0, None, ALU.add))
                    dve.scalar_tensor_tensor(out=U[s][:, :, :], in0=U[s][:, :, :], scalar=1.0, in1=E,
                                             op0=ALU.subtract, op1=ALU.subtract).then_inc(xc_free, 1)
                    dve.wait_ge(xc_free, c + 2)
                    chain.step(dve.tensor_tensor(DT[s][:, :, :], DT[s][:, :, :], U[s][:, :, :], ALU.subtract))
                    dve.scalar_tensor_tensor(out=DT[s][:, :, :], in0=XV[:, :, :], scalar=0.0,
                                             in1=DT[s][:, :, :], op0=ALU.max, op1=ALU.add).then_inc(dt_done, 1)

                def gated(c, s, j):
                    if j == 0:
                        dve.wait_ge(w_ps, c * 2 + 2)
                    dve.wait_ge(y_done, c * UNITS + (UNITS - JT + j + 3))
                    dve.scalar_tensor_tensor(out=Z[:, j, :], in0=XS[s][:, j, :], scalar=DS[:, j:j + 1],
                                             in1=pY[j][:, :], op0=ALU.mult, op1=ALU.add
                                             ).then_inc(z_raw, 1)
                    dve.wait_ge(z_raw, c * JT + (JT + j + 1))
                    dve.tensor_tensor(Z[:, j, :], Z[:, j, :], GT[s][:, j, :], ALU.mult
                                      ).then_inc(z_done, 1)

                chain = Chain(dve, steps_s)
                dve.sem_inc(xc_free, 1)
                dve.sem_inc(scanned, 2)
                dve.sem_inc(hc_done, 8)
                dve.sem_inc(z_raw, JT)
                chain.step(dve.memset(MK[:, :], 1.0))
                for b in range(batches):
                    chain.step(dve.memset(MK[:, b * CB:b * CB + 1], 0.0))
                chain.step(dve.memset(HS[:, :, :], 0.0))
                chain.step(dve.memset(CR[:, :, :], 0.0))
                dve.wait_ge(w_ld, 16 * 9)
                dve.wait_ge(a_ready, 1)
                dve.tensor_scalar(AN[:, :, :], AN[:, :, :], -1.0, None, ALU.mult).then_inc(ready, 1)
                made = chain.n
                chain.at(made)
                conv(0, 0, chain)
                softplus(0, 0, chain)
                PER = chain.n

                def body(c, u, s, first, last, more):
                    dve.tensor_scalar(HS[:, :, :], HS[:, :, :], MK[:, ds(c, 1)], None, ALU.mult
                                      ).then_inc(hs_kept, 1)
                    dve.wait_ge(hs_kept, c * (UNITS + 1) + 1)
                    chain.at(c * PER + (made + PER))
                    for k in range(UNITS):
                        q, j = divmod(k, JT)
                        h = H[k % 2]
                        dve.wait_ge(da_done, c * UNITS + (k + 1))
                        dve.wait_ge(db_done, c * UNITS + (k + 9))
                        dve.wait_ge(y_done, c * UNITS + (k + 1))
                        for n in range(QN):
                            ins = dve.tensor_tensor_scan(h[:, n, :], DA[k % 2][:, n, :], DB[k % 2][:, n, :],
                                                         HS[:, j, q * QN + n:q * QN + n + 1],
                                                         ALU.mult, ALU.add)
                        ins.then_inc(scanned, 1)
                        dve.wait_ge(scanned, c * UNITS + (k + 3))
                        dve.tensor_copy(HS[:, j, q * QN:(q + 1) * QN], h[:, :, BANK - 1]
                                        ).then_inc(hs_kept, 1)
                        dve.wait_ge(hs_kept, c * (UNITS + 1) + (k + 2))
                        if j == 0:
                            dve.wait_ge(c_in[q % 2], c * 32 + (16 * (q // 2) + 16))
                        dve.tensor_tensor(h[:, :, :], h[:, :, :], BQ[q % 2][:, 1, :, :], ALU.mult
                                          ).then_inc(hc_done, 1)
                        if not last and k == 2:
                            conv(c + 1, 1 - s, chain)
                        if k == 0 and not first:
                            gated(c - 1, 1 - s, JT - 1)
                        if k > UNITS - JT:
                            gated(c, s, k - (UNITS - JT + 1))
                        if not last and k == 12:
                            softplus(c + 1, 1 - s, chain)
                    if last:
                        gated(c, s, JT - 1)
                bodies(dve, body)


def phase_route(nc, x, xn_d, mo_d, oraw_d, wo, bo, g2, b2, gate_w, gate_b, slots_d, BASE, SLOT, TE, batches):
    T, C = x.shape
    NT, KC, TG = T // P, C // P, BANK // P
    NB = T // batches // BANK
    NE = gate_w.shape[1]
    NTL = TE.shape[1]
    GB = HEADS // GH
    QC = NB
    with ExitStack() as ctx:
        m = Place(nc, ctx, "route")
        WO = m.sb("wo", [P, KC, C])
        BO = m.sb("bo", [1, C])
        GW = m.sb("gw", [P, KC, NE])
        GBI = m.sb("gb", [1, NE])
        G = m.sb("g", [P, C])
        B = m.sb("b", [P, C])
        ONE = m.sb("one", [1, P])
        ident = m.sb("ident", [P, P])
        LOWER = m.sb("lower", [P, P])
        ALL = m.sb("all", [P, P])
        OT = [m.sb(f"ot{s}", [P, KC, BANK]) for s in range(2)]
        SM = [m.sb(f"sm{s}", [P, KC, BANK]) for s in range(2)]
        XN = [m.sb(f"xn{s}", [P, TG, C]) for s in range(2)]
        XR = [m.sb(f"xr{s}", [P, 2, TG, C]) for s in range(2)]
        X1 = m.sb("x1", [P, NT, C])
        HN = m.sb("hn", [P, NT, C])
        ST = m.sb("stats", [P, NT, 6])
        MV = m.sb("meanvar", [P, NT, 2])
        V, ROOT, RS, TMP = (m.sb(n, [P, NT]) for n in ("var", "root", "rstd", "tmp"))
        HT = [m.sb(f"ht{n}", [P, KC, P]) for n in range(2)]
        LG, EQ, OH, TOT, INC, POS = (m.sb(n, [P, NT, NE]) for n in ("lg", "eq", "oh", "tot", "inc", "pos"))
        WT = m.sb("wt", [P, NE])
        MXL = m.sb("mxl", [P, NT])
        MW = m.sb("mw", [P, NT])
        CNT, NBF, BEND, BST = (m.sb(n, [P, NE]) for n in ("cnt", "nbf", "bend", "bst"))
        CNTI = m.sb("cnti", [P, NE], I32)
        UNIT = m.sb("unit", [P, max(NT, NE)])
        JT = m.sb("jt", [P, NTL])
        CMP = m.sb("cmp", [P, NTL, NE])
        TEF = m.sb("tef", [P, NTL])
        pA = [m.ps(f"pA{n}", [P, BANK]) for n in range(2)]
        pT = [m.ps(f"pT{n}", [P, KC * P]) for n in range(2)]
        pG = m.ps("pG", [P, NT, NE])
        pC = m.ps("pC", [P, NT, NE])
        pN = m.ps("pN", [P, NT, NE])
        w_in = m.sem("w_in")
        id_ready = m.sem("id_ready")
        consts = m.sem("consts")
        o_in = [m.sem(f"o_in{s}") for s in range(2)]
        scale_s = m.sem("scale")
        a_ps = m.sem("a_ps")
        x1_done = m.sem("x1_done")
        stats = m.sem("stats")
        base_s = m.sem("base")
        chain_s = m.sem("chain")
        var_ready = m.sem("var_ready")
        root_ready = m.sem("root_ready")
        hn_raw = m.sem("hn_raw")
        hn_mul = m.sem("hn_mul")
        hn_done = m.sem("hn_done")
        t_ps = m.sem("t_ps")
        t_sb = m.sem("t_sb")
        g_ps = m.sem("g_ps")
        oh_done = m.sem("oh_done")
        n_ps = m.sem("n_ps")
        slot_done = m.sem("slot_done")
        sent = m.sem("sent")

        def chunks(eng, body):
            with eng.Fori(0, batches) as b:
                with eng.Fori(0, NB // 2) as i:
                    for s in range(2):
                        body(b * NB + i * 2 + s, b * (NB // 2) + i, s, b, i * 2 + s)

        with nc.Block() as block:

            @block.sync
            def _(sp):
                for dst, src in ((WO[:, :, :], wo.rearrange("(k p) n -> p k n", p=P)),
                                 (BO[:, :], bo.rearrange("(o n) -> o n", o=1)),
                                 (GW[:, :, :], gate_w.rearrange("(k p) n -> p k n", p=P)),
                                 (GBI[:, :], gate_b.rearrange("(o n) -> o n", o=1)),
                                 (G[:, :], bcast_rows(g2, P)), (B[:, :], bcast_rows(b2, P))):
                    sp.dma_start(dst, src).then_inc(w_in, 16)

                def body(c, u, s, b, cb):
                    sp.wait_ge(base_s, c * 2 + 4)
                    for k in range(KC):
                        for g in range(2):
                            raw = oraw_d[ds(b * (GB * QC) + (2 * k + g) * QC + cb, 1), :, :] \
                                .rearrange("i (h r) q -> h (i r) q", r=P // GH)
                            half = slice(g * GH * HD, (g + 1) * GH * HD)
                            sp.dma_start(OT[s][half, k, :], raw[:, 0:HD, :]).then_inc(o_in[s], 16)
                            sp.dma_start(SM[s][half, k, :],
                                         raw[:, HD:VW, :].to_broadcast([GH, HD, BANK])).then_inc(o_in[s], 16)
                    rows = ds(c * BANK, BANK)
                    sp.dma_start(XN[s][:, :, :], xn_d[rows, :].rearrange("(t p) c -> p t c", p=P)
                                 ).then_inc(o_in[s], 16)
                    for n, src in enumerate((x, mo_d)):
                        sp.dma_start(XR[s][:, n, :, :], src[rows, :].rearrange("(t p) c -> p t c", p=P)
                                     ).then_inc(o_in[s], 16)
                chunks(sp, body)

            @block.gpsimd
            def _(pool):
                make_identity(pool, ident, id_ready)
                pool.iota(JT[:, :], pattern=[[1, NTL]], base=0, channel_multiplier=0,
                          allow_small_or_imprecise_dtypes=True).then_inc(consts, 1)
                pool.iota(WT[:, :], pattern=[[-1, NE]], base=NE, channel_multiplier=0,
                          allow_small_or_imprecise_dtypes=True).then_inc(consts, 1)
                pool.wait_ge(consts, 5)
                pool.affine_select(out=LOWER[:, :], in_=ALL[:, :], compare_op=ALU.is_gt, fill=0.0, base=0,
                                   pattern=[[1, P]], channel_multiplier=-1).then_inc(consts, 1)
                pool.sem_inc(base_s, 4)

                def body(c, u, s, b, cb):
                    pool.wait_ge(o_in[s], u * 176 + 176)
                    pool.tensor_tensor(XR[s][:, 0, :, :], XR[s][:, 0, :, :], XR[s][:, 1, :, :], ALU.add
                                       ).then_inc(base_s, 1)
                    pool.wait_ge(base_s, c * 2 + 5)
                    pool.wait_ge(x1_done, c * TG + TG)
                    pool.tensor_tensor(BASE[:, ds(c * TG, TG), :], XR[s][:, 0, :, :],
                                       X1[:, ds(c * TG, TG), :], ALU.add).then_inc(base_s, 1)
                chunks(pool, body)
                for g in range(NT // TG):
                    h = HN[:, g * TG:(g + 1) * TG, :]
                    pool.wait_ge(hn_raw, (g + 1) * TG)
                    pool.tensor_tensor(h, h, G[:, :].unsqueeze(1).to_broadcast([P, TG, C]), ALU.mult
                                       ).then_inc(hn_mul, 1)
                    pool.wait_ge(hn_mul, g + 1)
                    pool.tensor_tensor(h, h, B[:, :].unsqueeze(1).to_broadcast([P, TG, C]), ALU.add
                                       ).then_inc(hn_done, 1)
                pool.wait_ge(slot_done, 1)
                for t in range(NT):
                    pool.indirect_dma_start(out=slots_d, out_offset=bass.IndirectOffsetOnAxis(
                        ap=SLOT[:, t:t + 1], axis=0), in_=HN[:, t, :], in_offset=None).then_inc(sent, 16)
                pool.wait_ge(sent, 16 * NT)

            @block.tensor
            def _(pe):
                pe.wait_ge(w_in, 16 * 6)
                pe.wait_ge(id_ready, 2)
                pe.wait_ge(consts, 6)

                def body(c, u, s, b, cb):
                    pe.wait_ge(scale_s, c * 2 + 2)
                    for t in range(TG):
                        pe.wait_ge(stats, c * TG + (t + 1))
                        for k in range(KC):
                            pe.matmul(pA[t % 2][:, 0:C], OT[s][:, k, t * P:(t + 1) * P], WO[:, k, :],
                                      start=(k == 0), stop=False)
                        pe.matmul(pA[t % 2][:, 0:C], ONE[:, :], BO[:, :], start=False, stop=True
                                  ).then_inc(a_ps, 1)
                chunks(pe, body)

                def gate(t):
                    pe.wait_ge(t_sb, t + 1)
                    for k in range(KC):
                        pe.matmul(pG[:, t, :], HT[t % 2][:, k, :], GW[:, k, :], start=(k == 0), stop=False)
                    pe.matmul(pG[:, t, :], ONE[:, :], GBI[:, :], start=False, stop=True).then_inc(g_ps, 1)

                for t in range(NT):
                    if t % TG == 0:
                        pe.wait_ge(hn_done, t // TG + 1)
                    if t >= 2:
                        pe.wait_ge(t_sb, t - 1)
                    for k in range(KC):
                        mm = pe.transpose(pT[t % 2][:, k * P:(k + 1) * P], HN[:, t, k * P:(k + 1) * P],
                                          ident[:, :])
                    mm.then_inc(t_ps, 1)
                    if t >= 1:
                        gate(t - 1)
                gate(NT - 1)
                pe.wait_ge(oh_done, 1)
                pe.matmul(pC[:, :, :], LOWER[:, :], OH[:, :, :], start=True, stop=True).then_inc(n_ps, 1)
                pe.matmul(pN[:, :, :], ALL[:, :], OH[:, :, :], start=True, stop=True).then_inc(n_ps, 1)

            @block.scalar
            def _(act):
                act.wait_ge(var_ready, 1)
                act.activation(ROOT[:, :], V[:, :], ACT.Sqrt).then_inc(root_ready, 1)
                for t in range(NT):
                    act.wait_ge(t_ps, t + 1)
                    if t >= 2:
                        act.wait_ge(g_ps, t - 1)
                    act.copy(HT[t % 2][:, :, :], pT[t % 2][:, :]).then_inc(t_sb, 1)

            @block.vector
            def _(dve):
                chain = Chain(dve, chain_s)
                dve.memset(ONE[:, :], 1.0).then_inc(consts, 1)
                dve.memset(ALL[:, :], 1.0).then_inc(consts, 1)
                dve.memset(UNIT[:, :], 1.0).then_inc(consts, 1)
                dve.sem_inc(stats, 2)

                def body(c, u, s, b, cb):
                    dve.wait_ge(o_in[s], u * 176 + 176)
                    dve.reciprocal(SM[s][:, :, :], SM[s][:, :, :]).then_inc(scale_s, 1)
                    dve.wait_ge(scale_s, c * 2 + 1)
                    dve.tensor_tensor(OT[s][:, :, :], OT[s][:, :, :], SM[s][:, :, :], ALU.mult
                                      ).then_inc(scale_s, 1)
                    for t in range(TG):
                        row = X1[:, ds(c * TG + t, 1), :]
                        dve.wait_ge(a_ps, c * TG + (t + 1))
                        dve.tensor_tensor(row, pA[t % 2][:, 0:C].unsqueeze(1), XN[s][:, t:t + 1, :], ALU.add
                                          ).then_inc(x1_done, 1)
                        dve.wait_ge(x1_done, c * TG + (t + 1))
                        dve.bn_stats(ST[:, ds(c * TG + t, 1), :], row).then_inc(stats, 1)
                chunks(dve, body)
                dve.wait_ge(stats, NT + 2)
                for t in range(NT):
                    dve.bn_aggr(MV[:, t, :], ST[:, t, :]).then_inc(stats, 1)
                dve.wait_ge(stats, 2 * NT + 2)
                chain.step(dve.tensor_copy(V[:, :], MV[:, :, 1]))
                rstd_steps(dve, chain, V[:, :], ROOT[:, :], RS[:, :], TMP[:, :], var_ready, root_ready, 1)
                with dve.Fori(0, NT) as t:
                    dve.tensor_scalar(HN[:, ds(t, 1), :], X1[:, ds(t, 1), :], MV[:, ds(t, 1), 0:1],
                                      RS[:, ds(t, 1)], ALU.subtract, ALU.mult).then_inc(hn_raw, 1)

                def over_e(ap):
                    return ap.unsqueeze(2).to_broadcast([P, NT, NE])

                def over_t(ap):
                    return ap.unsqueeze(1).to_broadcast([P, NT, NE])

                dve.wait_ge(consts, 6)
                dve.wait_ge(g_ps, NT)
                chain.step(dve.tensor_copy(LG[:, :, :], pG[:, :, :]))
                chain.step(dve.tensor_reduce(MXL[:, :], LG[:, :, :], AX.X, ALU.max))
                chain.step(dve.tensor_tensor(EQ[:, :, :], LG[:, :, :], over_e(MXL[:, :]), ALU.is_equal))
                chain.step(dve.tensor_tensor(EQ[:, :, :], EQ[:, :, :], over_t(WT[:, :]), ALU.mult))
                chain.step(dve.tensor_reduce(MW[:, :], EQ[:, :, :], AX.X, ALU.max))
                chain.step(dve.tensor_copy(EQ[:, :, :], over_t(WT[:, :])))
                dve.tensor_tensor(OH[:, :, :], EQ[:, :, :], over_e(MW[:, :]), ALU.is_equal
                                  ).then_inc(oh_done, 1)
                dve.wait_ge(n_ps, 2)
                dve.wait_ge(oh_done, 1)
                chain.step(dve.tensor_copy(TOT[:, :, :], pN[:, :, :]))
                for e in range(NE):
                    ins = dve.tensor_tensor_scan(INC[:, :, e], UNIT[:, 0:NT], TOT[:, :, e], 0.0,
                                                 ALU.mult, ALU.add)
                chain.step(ins)
                chain.step(dve.tensor_tensor(POS[:, :, :], INC[:, :, :], TOT[:, :, :], ALU.subtract))
                chain.step(dve.tensor_tensor(POS[:, :, :], POS[:, :, :], pC[:, :, :], ALU.add))
                chain.step(dve.tensor_scalar(CNT[:, :], INC[:, NT - 1, :], float(MT - 1), None, ALU.add))
                chain.step(dve.tensor_copy(CNTI[:, :], CNT[:, :]))
                chain.step(dve.tensor_scalar(CNTI[:, :], CNTI[:, :], MT.bit_length() - 1, None,
                                             ALU.logical_shift_right))
                chain.step(dve.tensor_copy(NBF[:, :], CNTI[:, :]))
                chain.step(dve.tensor_tensor_scan(BEND[:, :], UNIT[:, 0:NE], NBF[:, :], 0.0, ALU.mult, ALU.add))
                chain.step(dve.tensor_tensor(BST[:, :], BEND[:, :], NBF[:, :], ALU.subtract))
                chain.step(dve.scalar_tensor_tensor(out=POS[:, :, :], in0=over_t(BST[:, :]), scalar=float(MT),
                                                    in1=POS[:, :, :], op0=ALU.mult, op1=ALU.add))
                chain.step(dve.tensor_tensor(POS[:, :, :], POS[:, :, :], OH[:, :, :], ALU.mult))
                chain.step(dve.tensor_reduce(MW[:, :], POS[:, :, :], AX.X, ALU.add))
                dve.tensor_copy(SLOT[:, :], MW[:, :]).then_inc(slot_done, 1)
                shape = [P, NTL, NE]
                chain.step(dve.tensor_tensor(CMP[:, :, :], JT[:, :].unsqueeze(2).to_broadcast(shape),
                                             BEND[:, :].unsqueeze(1).to_broadcast(shape), ALU.is_ge))
                chain.step(dve.tensor_reduce(TEF[:, :], CMP[:, :, :], AX.X, ALU.add))
                chain.step(dve.tensor_scalar(TEF[:, :], TEF[:, :], float(NE - 1), None, ALU.min))
                chain.step(dve.tensor_copy(TE[:, :], TEF[:, :]))


def phase_experts(nc, w1, b1, w2, b2, slots_d, ys_d, TE):
    E, C, F = w1.shape
    NTL = TE.shape[1]
    KC, KF, TT = C // P, F // P, MT // P
    with ExitStack() as ctx:
        m = Place(nc, ctx, "exp")
        W1 = [m.sb(f"w1{s}", [P, KC, F]) for s in range(2)]
        W2 = [m.sb(f"w2{s}", [P, KF, C]) for s in range(2)]
        B1 = [m.sb(f"b1{s}", [P, KF]) for s in range(2)]
        B2 = [m.sb(f"b2{s}", [1, C]) for s in range(2)]
        XR = [m.sb(f"xr{s}", [P, TT, C]) for s in range(2)]
        XT = [m.sb(f"xt{s}", [P, KC, MT]) for s in range(2)]
        HM = [m.sb(f"hm{s}", [P, KF, MT]) for s in range(2)]
        YO = [m.sb(f"yo{s}", [P, TT, C]) for s in range(2)]
        ONE = m.sb("one", [1, P])
        ident = m.sb("ident", [P, P])
        pT = [m.ps(f"pT{n}", [P, KC, MT]) for n in range(2)]
        pH = [m.ps(f"pH{n}", [P, 2, MT]) for n in range(KF // 2)]
        pY = [m.ps(f"pY{n}", [P, TT, C]) for n in range(2)]
        id_ready = m.sem("id_ready")
        one_ready = m.sem("one_ready")
        x_in = [m.sem(f"x_in{s}") for s in range(2)]
        w1_in = [m.sem(f"w1_in{s}") for s in range(2)]
        w2_in = [m.sem(f"w2_in{s}") for s in range(2)]
        x_ps = m.sem("x_ps")
        x_sb = m.sem("x_sb")
        h_ps = m.sem("h_ps")
        h_act = m.sem("h_act")
        h_dve = m.sem("h_dve")
        y_ps = m.sem("y_ps")
        y_sb = m.sem("y_sb")
        y_out = [m.sem(f"y_out{s}") for s in range(2)]
        NH = KF // 2

        def bodies(eng, body):
            pairs = (NTL - 1) // 2
            with eng.Fori(0, pairs) as i:
                for s in range(2):
                    body(i * 2 + s, i, s, False)
            for j in range(2 * pairs, NTL):
                body(j, j // 2, j % 2, j == NTL - 1)

        with nc.Block() as block:

            @block.sync
            def _(sp):
                def load(j, s):
                    e = sp.value_load(TE[0:1, ds(j, 1)], min_val=0, max_val=E - 1)
                    sp.dma_start(XR[s][:, :, :],
                                 slots_d[ds(j * MT, MT), :].rearrange("(t p) c -> p t c", p=P)
                                 ).then_inc(x_in[s], 16)
                    sp.dma_start(W1[s][:, :, :], w1[ds(e, 1), :, :].rearrange("e (k p) f -> p (e k) f", p=P)
                                 ).then_inc(w1_in[s], 16)
                    sp.dma_start(B1[s][:, :], b1[ds(e, 1), :, :].rearrange("e p k -> (e p) k")
                                 ).then_inc(w1_in[s], 16)
                    sp.dma_start(W2[s][:, :, :], w2[ds(e, 1), :, :].rearrange("e (k p) c -> p (e k) c", p=P)
                                 ).then_inc(w2_in[s], 16)
                    sp.dma_start(B2[s][:, :], b2[ds(e, 1), :]).then_inc(w2_in[s], 16)

                for s in range(2):
                    sp.sem_inc(y_out[s], 16)
                load(0, 0)

                def body(j, u, s, last):
                    if not last:
                        sp.wait_ge(y_ps, j + 2)
                        sp.wait_ge(h_act, j * (NH // 2) + NH // 2)
                        sp.wait_ge(h_dve, j * (NH // 2) + NH // 2)
                        load(j + 1, 1 - s)
                    sp.wait_ge(y_sb, j + 3)
                    sp.dma_start(ys_d[ds(j * MT, MT), :].rearrange("(t p) c -> p t c", p=P),
                                 YO[s][:, :, :]).then_inc(y_out[s], 16)
                bodies(sp, body)
                sp.wait_ge(y_out[0], 16 * ((NTL + 1) // 2 + 1))
                sp.wait_ge(y_out[1], 16 * (NTL // 2 + 1))

            @block.gpsimd
            def _(pool):
                make_identity(pool, ident, id_ready)

            @block.tensor
            def _(pe):
                def turn(j, u, s):
                    pe.wait_ge(x_in[s], u * 16 + 16)
                    pe.wait_ge(x_sb, j + 1)
                    for k in range(KC):
                        for t in range(TT):
                            mm = pe.transpose(pT[s][:, k, t * P:(t + 1) * P],
                                              XR[s][:, t, k * P:(k + 1) * P], ident[:, :])
                    mm.then_inc(x_ps, 1)

                pe.sem_inc(y_ps, 2)
                pe.wait_ge(id_ready, 2)
                pe.wait_ge(one_ready, 1)
                turn(0, 0, 0)

                def body(j, u, s, last):
                    pe.wait_ge(x_sb, j + 3)
                    pe.wait_ge(w1_in[s], u * 32 + 32)
                    for n in range(NH):
                        pe.wait_ge((h_act, h_dve)[n % 2], j * (NH // 2) + (n // 2 + 1))
                        for f in range(2 * n, 2 * n + 2):
                            for k in range(KC):
                                mm = pe.matmul(pH[n][:, f % 2, :], W1[s][:, k, f * P:(f + 1) * P],
                                               XT[s][:, k, :], start=(k == 0), stop=(k == KC - 1))
                        mm.then_inc(h_ps, 1)
                    if not last:
                        turn(j + 1, u + s, 1 - s)
                    pe.wait_ge(w2_in[s], u * 32 + 32)
                    pe.wait_ge(y_sb, j + 1)
                    for t in range(TT):
                        for f in range(KF):
                            if t == 0 and f % 2 == 0:
                                n = f // 2
                                pe.wait_ge((h_act, h_dve)[n % 2], j * (NH // 2) + (NH // 2 + n // 2 + 1))
                            pe.matmul(pY[s][:, t, :], HM[s][:, f, t * P:(t + 1) * P], W2[s][:, f, :],
                                      start=(f == 0), stop=False)
                        mm = pe.matmul(pY[s][:, t, :], ONE[:, :], B2[s][:, :], start=False, stop=True)
                    mm.then_inc(y_ps, 1)
                bodies(pe, body)

            @block.scalar
            def _(act):
                act.sem_inc(h_act, NH // 2)
                act.sem_inc(y_sb, 2)

                def body(j, u, s, last):
                    act.wait_ge(w1_in[s], u * 32 + 32)
                    for n in range(0, NH, 2):
                        act.wait_ge(h_ps, j * NH + (n + 1))
                        act.activation(HM[s][:, 2 * n, :], pH[n][:, 0, :], ACT.Relu,
                                       bias=B1[s][:, 2 * n:2 * n + 1])
                        act.activation(HM[s][:, 2 * n + 1, :], pH[n][:, 1, :], ACT.Relu,
                                       bias=B1[s][:, 2 * n + 1:2 * n + 2]).then_inc(h_act, 1)
                    act.wait_ge(y_ps, j + 3)
                    act.wait_ge(y_out[s], u * 16 + 16)
                    act.copy(YO[s][:, :, :], pY[s][:, :, :]).then_inc(y_sb, 1)
                bodies(act, body)

            @block.vector
            def _(dve):
                dve.memset(ONE[:, :], 1.0).then_inc(one_ready, 1)
                dve.sem_inc(x_sb, 2)
                dve.sem_inc(h_dve, NH // 2)

                def turned(j, s):
                    dve.wait_ge(x_ps, j + 1)
                    dve.tensor_copy(XT[s][:, :, :], pT[s][:, :, :]).then_inc(x_sb, 1)

                turned(0, 0)

                def body(j, u, s, last):
                    dve.wait_ge(w1_in[s], u * 32 + 32)
                    for n in range(1, NH, 2):
                        dve.wait_ge(h_ps, j * NH + (n + 1))
                        dve.tensor_scalar(HM[s][:, 2 * n, :], pH[n][:, 0, :], B1[s][:, 2 * n:2 * n + 1], 0.0,
                                          ALU.add, ALU.max)
                        dve.tensor_scalar(HM[s][:, 2 * n + 1, :], pH[n][:, 1, :],
                                          B1[s][:, 2 * n + 1:2 * n + 2], 0.0, ALU.add, ALU.max
                                          ).then_inc(h_dve, 1)
                    if not last:
                        turned(j + 1, 1 - s)
                bodies(dve, body)


def phase_output(nc, ys_d, out, BASE, SLOT):
    T, C = out.shape
    NT, TG = T // P, BANK // P
    with ExitStack() as ctx:
        m = Place(nc, ctx, "out")
        Y = m.sb("y", [P, NT, C])
        got = [m.sem(f"got{g}") for g in range(NT // TG)]
        added = m.sem("added")
        stored = m.sem("stored")

        with nc.Block() as block:

            @block.gpsimd
            def _(pool):
                for t in range(NT):
                    pool.indirect_dma_start(out=Y[:, t, :], out_offset=None, in_=ys_d,
                                            in_offset=bass.IndirectOffsetOnAxis(ap=SLOT[:, t:t + 1], axis=0)
                                            ).then_inc(got[t // TG], 16)

            @block.vector
            def _(dve):
                for g in range(NT // TG):
                    rows = slice(g * TG, (g + 1) * TG)
                    dve.wait_ge(got[g], 16 * TG)
                    dve.tensor_tensor(Y[:, rows, :], Y[:, rows, :], BASE[:, rows, :], ALU.add).then_inc(added, 1)

            @block.sync
            def _(sp):
                for g in range(NT // TG):
                    sp.wait_ge(added, g + 1)
                    sp.dma_start(out[g * BANK:(g + 1) * BANK, :].rearrange("(t p) c -> p t c", p=P),
                                 Y[:, g * TG:(g + 1) * TG, :]).then_inc(stored, 16)
                sp.wait_ge(stored, 16 * (NT // TG))


def build(nc, a, out, batches):
    x = a["x"]
    T, C = x.shape
    L = T // batches
    NCH = T // BANK
    E = a["w1"].shape[0]
    N2 = a["w_x"].shape[1] - a["w_dt"].shape[0]
    NTL = T // MT + E - 1

    def scratch(name, shape, dt=F32):
        return nc.dram_tensor(name, shape, dt).ap()

    xn_d = scratch("xn_d", [T, C])
    hn_d = scratch("hn_d", [T, C])
    xnT_d = scratch("xnT_d", [C, T])
    parts_d = scratch("parts_d", [2, 3, batches * C, L], BF16)
    v_d = scratch("v_d", [batches * HEADS // GH, L, GH * VW])
    bc_d = scratch("bc_d", [NCH, N2, BANK])
    mo_d = scratch("mo_d", [T, C])
    oraw_d = scratch("oraw_d", [batches * HEADS // GH * (L // BANK), P, BANK])
    slots_d = scratch("slots_d", [NTL * MT, C])
    ys_d = scratch("ys_d", [NTL * MT, C])

    phase_norm(nc, x, a["ln1_g"], a["ln1_b"], xn_d, hn_d, slots_d)
    phase_project(nc, xn_d, hn_d, a["wq"], a["bq"], a["wk"], a["bk"], a["wv"], a["bv"],
                  xnT_d, parts_d, v_d, batches)
    phase_mamba(nc, xnT_d, a["w_in"], a["conv_w"], a["conv_b"], a["w_x"], a["w_dt"], a["b_dt"],
                a["a_log"], a["d_skip"], a["w_out"], bc_d, mo_d, batches)
    phase_attention(nc, parts_d, v_d, oraw_d, batches)
    with ExitStack() as ctx:
        m = Place(nc, ctx, "kept")
        BASE = m.sb("base", [P, T // P, C])
        SLOT = m.sb("slot", [P, T // P], I32)
        TE = m.sb("te", [P, NTL], I32)
        phase_route(nc, x, xn_d, mo_d, oraw_d, a["wo"], a["bo"], a["ln2_g"], a["ln2_b"],
                    a["gate_w"], a["gate_b"], slots_d, BASE, SLOT, TE, batches)
        phase_experts(nc, a["w1"], a["b1"], a["w2"], a["b2"], slots_d, ys_d, TE)
        phase_output(nc, ys_d, out, BASE, SLOT)


def lay_out(inputs):
    import numpy as np

    def whole(a):
        return np.ascontiguousarray(a)

    def tiles(a):
        a = np.asarray(a)
        a = a.reshape(a.shape[0] // P, P, -1)
        return whole(a.transpose(1, 0, 2).reshape(P, -1))

    t = {k: np.asarray(v) for k, v in inputs.items()}
    x = t["L0_attn_x"]
    mamba = {n: t[f"L0_attn_{k}"] for n, k in (("w_in", "W_in"), ("w_x", "W_x"), ("w_dt", "W_dt"),
                                               ("w_out", "W_out"))}
    mamba |= {n: tiles(t[f"L0_attn_{k}"]) for n, k in (("conv_w", "conv_w"), ("conv_b", "conv_b"),
                                                       ("b_dt", "b_dt"), ("a_log", "A_log"), ("d_skip", "D"))}
    ffn = {n: t[f"L0_ffn_{n}"] for n in ("ln1_g", "ln1_b", "ln2_g", "ln2_b", "wq", "wk", "wv", "bv", "wo",
                                         "bo", "gate_w", "gate_b", "w1", "w2", "b2")}
    ffn |= {n: tiles(t[f"L0_ffn_{n}"]) for n in ("bq", "bk")}
    b1 = t["L0_ffn_b1"]
    ffn["b1"] = whole(b1.reshape(b1.shape[0], -1, P).transpose(0, 2, 1))
    return {"x": whole(x.reshape(-1, x.shape[-1]))} | {k: whole(v) for k, v in (mamba | ffn).items()}


def kernel(**inputs):
    import concourse.bacc as bacc
    from concourse.bass_utils import run_bass_kernel_spmd

    shape = inputs["L0_attn_x"].shape
    arrays = lay_out(inputs)
    nc = bacc.Bacc("TRN2", target_bir_lowering=False, num_devices=1)
    args = {n: nc.dram_tensor(f"in_{n}", v.shape, mybir.dt.from_np(v.dtype), kind="ExternalInput").ap()
            for n, v in arrays.items()}
    out = nc.dram_tensor("out_0", list(arrays["x"].shape), F32, kind="ExternalOutput").ap()
    build(nc, args, out, shape[0])
    r = run_bass_kernel_spmd(nc, [{f"in_{n}": v for n, v in arrays.items()}], core_ids=[0])
    return r.results[0]["out_0"].reshape(shape)
```

```python
from contextlib import ExitStack

import concourse.bass as bass
from concourse import mybir

ALU = mybir.AluOpType
ACT = mybir.ActivationFunctionType
AX = mybir.AxisListType
F32 = mybir.dt.float32
BF16 = mybir.dt.bfloat16
I32 = mybir.dt.int32
ds = bass.ds

P = 128
BANK = 512
EPS = 1e-5
HEADS = 16
HD = 16
GH = 4
VW = HD + 1
STACK = 6 * HD
Q_PARTS = [0, 0, 1, 0, 2, 1]
K_PARTS = [0, 1, 0, 2, 0, 1]
MT = 256


class Place:

    def __init__(self, nc, ctx, phase):
        self.nc, self.ctx, self.phase = nc, ctx, phase

    def sb(self, name, shape, dt=F32):
        return self.ctx.enter_context(self.nc.sbuf_tensor(f"{self.phase}_{name}", shape, dt))

    def ps(self, name, shape, dt=F32):
        return self.ctx.enter_context(self.nc.psum_tensor(f"{self.phase}_{name}", shape, dt))

    def sem(self, name):
        return self.ctx.enter_context(self.nc.semaphore(f"{self.phase}_{name}"))


class Chain:

    def __init__(self, eng, sem):
        self.eng, self.sem, self.base, self.n = eng, sem, 0, 0

    def at(self, base):
        self.base, self.n = base, 0

    def step(self, ins):
        self.n += 1
        ins.then_inc(self.sem, 1)
        self.eng.wait_ge(self.sem, self.base + self.n)

    def mark(self, ins):
        self.n += 1
        ins.then_inc(self.sem, 1)

    def join(self):
        self.eng.wait_ge(self.sem, self.base + self.n)


def bcast_rows(ap, n):
    return ap.rearrange("(o c) -> o c", o=1).to_broadcast([n, ap.shape[0]])


def make_identity(pool, ident, sem):
    pool.memset(ident[:, :], 0.0).then_inc(sem, 1)
    pool.wait_ge(sem, 1)
    pool.affine_select(out=ident[:, :], in_=ident[:, :], compare_op=ALU.not_equal, fill=1.0,
                       base=0, pattern=[[-1, P]], channel_multiplier=1).then_inc(sem, 1)


def rstd_steps(dve, chain, var, root, r, tmp, var_ready, root_ready, n):
    dve.wait_ge(root_ready, n)
    dve.wait_ge(var_ready, n)
    chain.step(dve.reciprocal(r, root))
    chain.step(dve.tensor_tensor(tmp, r, r, ALU.mult))
    chain.step(dve.tensor_tensor(tmp, tmp, var, ALU.mult))
    chain.step(dve.tensor_scalar(tmp, tmp, -0.5, 1.5, ALU.mult, ALU.add))
    chain.step(dve.tensor_tensor(r, r, tmp, ALU.mult))


def phase_project(nc, x, g1, b1, wq, bq, wk, bk, wv, bv, xn_d, xnT_d, parts_d, v_d, batches):
    T, C = x.shape
    KC = C // P
    TG = BANK // P
    NB = T // batches // BANK
    GB = HEADS // GH
    assert NB % 2 == 0
    with ExitStack() as ctx:
        m = Place(nc, ctx, "proj")
        X = [m.sb(f"x{s}", [P, TG, C]) for s in range(2)]
        HN = [m.sb(f"hn{s}", [P, TG, C]) for s in range(2)]
        ST = m.sb("stats", [P, TG, 6])
        MV = m.sb("meanvar", [P, TG, 2])
        V, ROOT, R, TMP = (m.sb(n, [P, TG]) for n in ("var", "root", "rstd", "tmp"))
        G = m.sb("g", [P, C])
        B = m.sb("b", [P, C])
        TR = [[m.sb(f"tr{s}{n}", [P, KC, BANK]) for n in range(2)] for s in range(2)]
        WQK = m.sb("wqk", [P, 2, KC, C])
        WV = m.sb("wv", [P, KC, C])
        BQK = m.sb("bqk", [P, 2, KC])
        BV = m.sb("bv", [1, C])
        ONE = m.sb("one", [1, P])
        ident = m.sb("ident", [P, P])
        QF = [m.sb(f"qf{n}", [P, BANK]) for n in range(2)]
        QR = [m.sb(f"qr{n}", [P, BANK]) for n in range(2)]
        QP = [m.sb(f"qp{n}", [P, 3, BANK], BF16) for n in range(2)]
        VS = [m.sb(f"vs{n}", [P, HEADS, VW]) for n in range(2)]
        pT = [m.ps(f"pT{n}", [P, BANK]) for n in range(4)]
        pQ = [m.ps(f"pQ{n}", [P, BANK]) for n in range(2)]
        pV = [m.ps(f"pV{n}", [P, BANK]) for n in range(2)]
        w_in = m.sem("w_in")
        id_ready = m.sem("id_ready")
        ones_ready = m.sem("ones_ready")
        x_in = [m.sem(f"x_in{s}") for s in range(2)]
        rows_used = [m.sem(f"rows_used{s}") for s in range(2)]
        norm_s = m.sem("norm")
        waited_v = m.sem("waited_v")
        waited_sp = m.sem("waited_sp")
        var_ready = m.sem("var_ready")
        root_ready = m.sem("root_ready")
        xn_done = m.sem("xn_done")
        xn_out = [m.sem(f"xn_out{s}") for s in range(2)]
        hn_raw = m.sem("hn_raw")
        hn_mul = m.sem("hn_mul")
        hn_done = m.sem("hn_done")
        turned = [m.sem(f"turned{n}") for n in range(2)]
        turned_sb = [m.sem(f"turned_sb{n}") for n in range(2)]
        xnT_out = [m.sem(f"xnT_out{s}") for s in range(2)]
        qk_ps = m.sem("qk_ps")
        qk_f = m.sem("qk_f")
        qk_hi = m.sem("qk_hi")
        qk_r = m.sem("qk_r")
        qk_mid = m.sem("qk_mid")
        qk_low = m.sem("qk_low")
        parts_out = [m.sem(f"parts_out{n}") for n in range(2)]
        v_ps = m.sem("v_ps")
        v_sb = m.sem("v_sb")
        v_out = [m.sem(f"v_out{n}") for n in range(2)]

        NCH = batches * NB

        def chunks(eng, body):
            for b in range(batches):
                pairs = NB // 2 - (b == batches - 1)
                if pairs:
                    with eng.Fori(0, pairs) as i:
                        for s in range(2):
                            body(b * NB + i * 2 + s, b * (NB // 2) + i, s, b, i * 2 + s, NCH)
            for s in range(2):
                body(NCH - 2 + s, NCH // 2 - 1, s, batches - 1, NB - 2 + s, 1 - s)

        with nc.Block() as block:

            @block.gpsimd
            def _(pool):
                make_identity(pool, ident, id_ready)

                def load_x(c, s):
                    pool.dma_start(X[s][:, :, :], x[ds(c * BANK, BANK), :].rearrange("(t p) c -> p t c", p=P)
                                   ).then_inc(x_in[s], 16)

                def scale(c, s):
                    pool.wait_ge(hn_raw, c + 1)
                    pool.tensor_tensor(HN[s][:, :, :], HN[s][:, :, :],
                                       G[:, :].unsqueeze(1).to_broadcast([P, TG, C]), ALU.mult
                                       ).then_inc(hn_mul, 1)
                    pool.wait_ge(hn_mul, c + 1)
                    pool.tensor_tensor(HN[s][:, :, :], HN[s][:, :, :],
                                       B[:, :].unsqueeze(1).to_broadcast([P, TG, C]), ALU.add
                                       ).then_inc(hn_done, 1)

                load_x(0, 0)
                load_x(1, 1)
                pool.wait_ge(w_in, 16 * 8)
                scale(0, 0)

                def body(c, u, s, b, cb, left):
                    if left >= 1:
                        scale(c + 1, 1 - s)
                    if left >= 2:
                        pool.wait_ge(rows_used[s], u + 2)
                        pool.wait_ge(xn_out[s], u * 16 + 16)
                        load_x(c + 2, s)
                chunks(pool, body)

            @block.sync
            def _(sp):
                for n, w in enumerate((wq, wk)):
                    sp.dma_start(WQK[:, n, :, :], w.rearrange("(k p) n -> p k n", p=P)).then_inc(w_in, 16)
                for n, w in enumerate((bq, bk)):
                    sp.dma_start(BQK[:, n, :], w).then_inc(w_in, 16)
                sp.dma_start(WV[:, :, :], wv.rearrange("(k p) n -> p k n", p=P)).then_inc(w_in, 16)
                sp.dma_start(BV[:, :], bv.rearrange("(o n) -> o n", o=1)).then_inc(w_in, 16)

                sp.dma_start(G[:, :], bcast_rows(g1, P)).then_inc(w_in, 16)
                sp.dma_start(B[:, :], bcast_rows(b1, P)).then_inc(w_in, 16)

                def store_xn(c, u, s):
                    sp.wait_ge(xn_done, c * TG + TG)
                    sp.dma_start(xn_d[ds(c * BANK, BANK), :].rearrange("(t p) c -> p t c", p=P),
                                 X[s][:, :, :]).then_inc(xn_out[s], 16)

                store_xn(0, 0, 0)

                def body(c, u, s, b, cb, left):
                    sp.wait_ge(turned_sb[0], c * KC + 2 * KC)
                    sp.sem_inc(waited_sp, 1)
                    sp.dma_start(xnT_d[:, ds(c * BANK, BANK)].rearrange("(k p) t -> p k t", p=P),
                                 TR[s][0][:, :, :]).then_inc(xnT_out[s], 16)
                    if left >= 1:
                        store_xn(c + 1, u + s, 1 - s)
                    for r in range(4):
                        qk, k = divmod(r, KC)
                        sp.wait_ge(qk_low, c * 4 + (r + 1))
                        sp.sem_inc(waited_sp, 1)
                        sp.dma_start(parts_d[qk][:, ds(b * C + k * P, P), ds(cb * BANK, BANK)]
                                     .rearrange("a r t -> r a t"), QP[r % 2][:, :, :]
                                     ).then_inc(parts_out[r % 2], 16)
                    for t in range(TG):
                        sp.wait_ge(v_sb, c * TG + (t + 3))
                        sp.dma_start(v_d[ds(b * GB, GB), ds(cb * BANK + t * P, P), :]
                                     .rearrange("g t x -> t g x"), VS[t % 2][:, :, :]
                                     ).then_inc(v_out[t % 2], 16)
                chunks(sp, body)
                n = batches * NB
                for s in range(2):
                    sp.wait_ge(xn_out[s], 16 * (n // 2))
                    sp.wait_ge(xnT_out[s], 16 * (n // 2 + 1))
                    sp.wait_ge(parts_out[s], 16 * (2 * n + 1))
                    sp.wait_ge(v_out[s], 16 * (2 * n + 1))

            @block.tensor
            def _(pe):
                for s in range(2):
                    pe.sem_inc(rows_used[s], 1)
                pe.wait_ge(w_in, 16 * 8)
                pe.wait_ge(id_ready, 2)
                pe.wait_ge(ones_ready, 3)

                def body(c, u, s, b, cb, left):
                    for n in range(2):
                        if n == 0:
                            pe.wait_ge(xn_done, c * TG + TG)
                        else:
                            pe.wait_ge(hn_done, c + 1)
                        for k in range(KC):
                            pe.wait_ge(turned_sb[n], c * KC + (k + 1))
                            for t in range(TG):
                                mm = pe.transpose(pT[2 * n + k][:, t * P:(t + 1) * P],
                                                  (X, HN)[n][s][:, t, k * P:(k + 1) * P], ident[:, :])
                            mm.then_inc(turned[n], 1)
                    pe.wait_ge(turned_sb[1], c * KC + 2 * KC)
                    pe.sem_inc(rows_used[s], 1)
                    for r in range(4):
                        qk, k = divmod(r, KC)
                        pe.wait_ge(qk_hi, c * 4 + (r + 1))
                        for kk in range(KC):
                            mm = pe.matmul(pQ[r % 2][:, :], WQK[:, qk, kk, k * P:(k + 1) * P],
                                           TR[s][1][:, kk, :], start=(kk == 0), stop=(kk == KC - 1))
                        mm.then_inc(qk_ps, 1)
                    for t in range(TG):
                        pe.wait_ge(v_sb, c * TG + (t + 1))
                        for kk in range(KC):
                            pe.matmul(pV[t % 2][:, 0:C], TR[s][1][:, kk, t * P:(t + 1) * P],
                                      WV[:, kk, :], start=(kk == 0), stop=False)
                        pe.matmul(pV[t % 2][:, 0:C], ONE[:, :], BV[:, :], start=False, stop=True
                                  ).then_inc(v_ps, 1)
                chunks(pe, body)

            @block.scalar
            def _(act):
                act.sem_inc(turned_sb[0], KC)
                act.sem_inc(qk_hi, 2)
                act.sem_inc(v_sb, 2)
                for s in range(2):
                    act.sem_inc(xnT_out[s], 16)
                    act.sem_inc(parts_out[s], 16)
                    act.sem_inc(v_out[s], 16)
                act.wait_ge(w_in, 16 * 8)
                act.wait_ge(ones_ready, 3)

                def root(c, n):
                    act.wait_ge(var_ready, c * 2 + (n + 1))
                    act.activation(ROOT[:, :], V[:, :], ACT.Sqrt).then_inc(root_ready, 1)

                root(0, 0)
                root(0, 1)

                def body(c, u, s, b, cb, left):
                    act.wait_ge(xnT_out[s], u * 16 + 16)
                    for k in range(KC):
                        act.wait_ge(turned[0], c * KC + (k + 1))
                        act.copy(TR[s][0][:, k, :], pT[k][:, :]).then_inc(turned_sb[0], 1)
                    for r in range(4):
                        qk, k = divmod(r, KC)
                        if r % 2 == 0 and left >= 1:
                            root(c + 1, r // 2)
                        act.wait_ge(qk_ps, c * 4 + (r + 1))
                        act.wait_ge(qk_r, c * 4 + (r + 1))
                        act.activation(QF[r % 2][:, :], pQ[r % 2][:, :], ACT.Identity,
                                       bias=BQK[:, qk, k:k + 1]).then_inc(qk_f, 1)
                        act.wait_ge(parts_out[r % 2], c * 32 + (16 * (r // 2) + 16))
                        act.activation(QP[r % 2][:, 0, :], pQ[r % 2][:, :], ACT.Identity,
                                       bias=BQK[:, qk, k:k + 1]).then_inc(qk_hi, 1)
                    for t in range(TG):
                        act.wait_ge(v_ps, c * TG + (t + 1))
                        act.wait_ge(v_out[t % 2], c * 32 + (16 * (t // 2) + 16))
                        act.copy(VS[t % 2][:, :, 0:HD],
                                 pV[t % 2][:, 0:C].rearrange("p (h d) -> p h d", d=HD)).then_inc(v_sb, 1)
                chunks(act, body)

            @block.vector
            def _(dve):
                dve.sem_inc(turned_sb[1], KC)
                dve.sem_inc(qk_r, 2)
                dve.memset(ONE[:, :], 1.0).then_inc(ones_ready, 1)
                for n in range(2):
                    dve.memset(VS[n][:, :, HD:VW], 1.0).then_inc(ones_ready, 1)

                chain = Chain(dve, norm_s)

                def variance(c, s, n):
                    for t in range(TG):
                        chain.mark(dve.bn_stats(ST[:, t, :], X[s][:, t, :]))
                    chain.join()
                    dve.sem_inc(waited_v, 1)
                    for t in range(TG):
                        chain.mark(dve.bn_aggr(MV[:, t, :], ST[:, t, :]))
                    chain.join()
                    dve.tensor_scalar(V[:, :], MV[:, :, 1], EPS, None, ALU.add).then_inc(var_ready, 1)

                def normalise(c, s, n):
                    rstd_steps(dve, chain, V[:, :], ROOT[:, :], R[:, :], TMP[:, :],
                               var_ready, root_ready, c * 2 + (n + 1))
                    for t in range(TG):
                        ins = dve.tensor_scalar((X, HN)[n][s][:, t, :], X[s][:, t, :], MV[:, t, 0:1],
                                                R[:, t:t + 1], ALU.subtract, ALU.mult)
                        if n == 0:
                            ins.then_inc(xn_done, 1)
                    if n == 1:
                        ins.then_inc(hn_raw, 1)

                def norm(c, u, s, part):
                    if part == 0:
                        dve.wait_ge(x_in[s], u * 16 + 16)
                        variance(c, s, 0)
                    if part == 1:
                        normalise(c, s, 0)
                        dve.wait_ge(xn_done, c * TG + TG)
                        variance(c, s, 1)
                    if part == 2:
                        dve.wait_ge(rows_used[s], u + 1)
                        normalise(c, s, 1)

                for part in range(3):
                    norm(0, 0, 0, part)
                PER = chain.n

                def body(c, u, s, b, cb, left):
                    chain.at(c * PER + PER)
                    if left >= 1:
                        norm(c + 1, u + s, 1 - s, 0)
                    for k in range(KC):
                        dve.wait_ge(turned[1], c * KC + (k + 1))
                        dve.tensor_copy(TR[s][1][:, k, :], pT[2 + k][:, :]).then_inc(turned_sb[1], 1)
                    for r in range(4):
                        n = r % 2
                        if n == 0 and left >= 1:
                            norm(c + 1, u + s, 1 - s, r // 2 + 1)
                        dve.wait_ge(qk_f, c * 4 + (r + 1))
                        dve.wait_ge(qk_hi, c * 4 + (r + 3))
                        dve.tensor_tensor(QR[n][:, :], QF[n][:, :], QP[n][:, 0, :], ALU.subtract
                                          ).then_inc(qk_r, 1)
                        dve.wait_ge(qk_r, c * 4 + (r + 3))
                        dve.tensor_copy(QP[n][:, 1, :], QR[n][:, :]).then_inc(qk_mid, 1)
                        dve.wait_ge(qk_mid, c * 4 + (r + 1))
                        dve.tensor_tensor(QP[n][:, 2, :], QR[n][:, :], QP[n][:, 1, :], ALU.subtract
                                          ).then_inc(qk_low, 1)
                chunks(dve, body)


def phase_attention(nc, parts_d, v_d, oraw_d, slots_d, batches):
    L = parts_d.shape[3]
    QC = L // BANK
    KT = L // P
    QT = BANK // P
    GC = GH * HD
    NG = batches * HEADS // GH
    NI = NG * QC
    RING = 4
    NSM = GH * QT * QC
    SM_KT = NSM // KT
    STACK_M = STACK + 3
    LOADS = 13
    SLOTS, ZR = slots_d.shape[0], 16 * P
    assert RING % QC == 0 and NI % RING == 0 and SM_KT * KT == NSM
    with ExitStack() as ctx:
        m = Place(nc, ctx, "attn")
        KS = [m.sb(f"ks{s}", [P, GH, L], BF16) for s in range(RING)]
        QS = [m.sb(f"qs{s}", [P, GH, BANK], BF16) for s in range(RING)]
        VS = [m.sb(f"vs{s}", [P, KT, GH, VW]) for s in range(RING)]
        PR = [m.sb(f"pr{n}", [P, 2, BANK]) for n in range(4)]
        OE = [m.sb(f"oe{n}", [P, BANK]) for n in range(2)]
        MX = m.sb("mx", [P, NSM])
        MN = m.sb("mn", [P, GH * QT])
        MR = m.sb("mr", [P, GH * QT])
        MS = m.sb("ms", [P, P // (GH * QT), GH * QT], BF16)
        MB = [m.sb(f"mb{n}", [P, P], BF16) for n in range(2)]
        ZERO = m.sb("zero", [P, slots_d.shape[1]])
        ident = m.sb("ident", [P, P])
        identb = m.sb("identb", [P, P], BF16)
        pS = [m.ps(f"pS{n}", [P, 2, BANK]) for n in range(2)]
        pX = [m.ps(f"pX{n}", [P, BANK]) for n in range(2)]
        pO = [m.ps(f"pO{n}", [P, BANK]) for n in range(2)]
        ops_in = [m.sem(f"ops_in{s}") for s in range(RING)]
        mrow_in = [m.sem(f"mrow_in{s}") for s in range(RING)]
        id_ready = m.sem("id_ready")
        ones_ready = m.sem("ones_ready")
        rest_zero = m.sem("rest_zero")
        zeroed = m.sem("zeroed")
        slots_out = m.sem("slots_out")
        x_ps = m.sem("x_ps")
        x_max = m.sem("x_max")
        mchain_s = m.sem("mchain")
        m_split = m.sem("m_split")
        m_ps = m.sem("m_ps")
        m_sb = m.sem("m_sb")
        s_ps = m.sem("s_ps")
        p_sb = m.sem("p_sb")
        pv_done = m.sem("pv_done")
        o_sb = m.sem("o_sb")
        o_out = [m.sem(f"o_out{n}") for n in range(2)]

        def turned_max(s):
            return pO[s % 2].bitcast(BF16)[:, 0:P]

        def where(i, s):
            i = i + s // RING if s >= RING else i
            s = s % RING
            return i * (RING // QC) + s // QC, s % QC, s, i

        def bodies(eng, body):
            if NI > RING:
                with eng.Fori(0, NI // RING - 1) as i:
                    for s in range(RING):
                        body(i, s, 9)
            for s in range(RING):
                body(NI // RING - 1, s, RING - 1 - s)

        with nc.Block() as block:

            @block.sync
            def _(sp):
                def load(i, s):
                    g, qc, slot, _ = where(i, s)
                    for a in range(6):
                        rows = slice(a * HD, (a + 1) * HD)
                        sp.dma_start(QS[slot][rows, :, :],
                                     parts_d[0, Q_PARTS[a]][ds(g * GC, GC), qc * BANK:(qc + 1) * BANK]
                                     .rearrange("(h c) t -> c h t", c=HD)).then_inc(ops_in[slot], 16)
                        sp.dma_start(KS[slot][rows, :, :],
                                     parts_d[1, K_PARTS[a]][ds(g * GC, GC), :]
                                     .rearrange("(h c) t -> c h t", c=HD)).then_inc(ops_in[slot], 16)
                    sp.dma_start(VS[slot][:, :, :, :],
                                 v_d[ds(g, 1), :, :].rearrange("g (k p) x -> p (g k) x", p=P)
                                 ).then_inc(ops_in[slot], 16)

                def max_rows(i, s):
                    _, _, slot, _ = where(i, s)
                    sp.wait_ge(m_sb, i * RING + (s + 1))
                    for a in range(3):
                        sp.dma_start(QS[slot][STACK + a:STACK + a + 1, :, :],
                                     MB[s % 2][a * GH * QT:(a + 1) * GH * QT, :]
                                     ).then_inc(mrow_in[slot], 16)

                for n in range(2):
                    sp.sem_inc(o_out[n], 32)
                for s in range(3):
                    load(0, s)
                max_rows(0, 0)
                sp.wait_ge(zeroed, 1)
                for r in range(0, SLOTS, ZR):
                    k = min(ZR, SLOTS - r) // P
                    sp.dma_start(slots_d[r:r + k * P, :].rearrange("(t p) c -> p t c", p=P),
                                 ZERO[:, :].unsqueeze(1).to_broadcast([P, k, slots_d.shape[1]])
                                 ).then_inc(slots_out, 16)

                def body(i, s, left):
                    if left >= 3:
                        sp.wait_ge(pv_done, i * (RING * KT) + (s * KT + 2))
                        load(i, s + 3)
                    if left >= 1:
                        max_rows(i, s + 1)
                    sp.wait_ge(o_sb, i * RING + (s + 3))
                    sp.dma_start(oraw_d[ds(i * RING + s, 1), :, :].rearrange("i p q -> p (i q)"),
                                 OE[s % 2][:, :]).then_inc(o_out[s % 2], 16)
                bodies(sp, body)
                sp.wait_ge(slots_out, 16 * -(-SLOTS // ZR))
                for n in range(2):
                    sp.wait_ge(o_out[n], 16 * (NI // 2 + 2))

            @block.gpsimd
            def _(pool):
                make_identity(pool, ident, id_ready)
                pool.wait_ge(id_ready, 2)
                for s in range(RING):
                    pool.memset(KS[s][STACK:STACK_M, :, :], 1.0).then_inc(ones_ready, 1)
                    pool.wait_ge(ones_ready, s + 1)

            @block.tensor
            def _(pe):
                def scores_max(i, s, n0, n1):
                    _, _, slot, use = where(i, s)
                    for n in range(n0, n1):
                        head, rest = divmod(n, QT * QC)
                        qt, part = divmod(rest, QC)
                        if n == 0:
                            pe.wait_ge(ops_in[slot], use * (16 * LOADS) + 16 * LOADS)
                        pe.wait_ge(x_max, i * (RING * NSM) + (s * NSM + n + 1))
                        pe.matmul(pX[n % 2][:, :], QS[slot][0:STACK, head, qt * P:(qt + 1) * P],
                                  KS[slot][0:STACK, head, part * BANK:(part + 1) * BANK],
                                  start=True, stop=True).then_inc(x_ps, 1)

                def max_turn(i, s):
                    pe.wait_ge(o_sb, i * RING + (s + 1))
                    pe.wait_ge(m_split, i * RING + (s + 1))
                    pe.transpose(turned_max(s), MS[:, :, :], identb[:, :]).then_inc(m_ps, 1)

                def scores(i, s, kt, pair):
                    _, _, slot, use = where(i, s)
                    if kt == 0 and pair == 0:
                        pe.wait_ge(mrow_in[slot], use * 48 + 48)
                    z = s * 2 * KT + kt * 2 + pair
                    pe.wait_ge(p_sb, i * (RING * 2 * KT) + (z + 1))
                    for h in range(2):
                        mm = pe.matmul(pS[pair][:, h, :],
                                       KS[slot][0:STACK_M, 2 * pair + h, kt * P:(kt + 1) * P],
                                       QS[slot][0:STACK_M, 2 * pair + h, :], start=True, stop=True)
                    mm.then_inc(s_ps, 1)

                def values(i, s, kt, half):
                    pe.wait_ge(p_sb, i * (RING * 2 * KT) + (s * 2 * KT + kt * 2 + half + 3))
                    for h in (2 * half, 2 * half + 1):
                        mm = pe.matmul(pO[s % 2][32 * h:32 * h + VW, :], VS[s][:, kt, h, :],
                                       PR[2 * (kt % 2) + half][:, h % 2, :],
                                       start=(kt == 0), stop=(kt == KT - 1))
                    if half == 1:
                        mm.then_inc(pv_done, 1)

                pe.sem_inc(pv_done, 2)
                pe.wait_ge(id_ready, 3)
                scores_max(0, 0, 0, NSM)
                pe.wait_ge(rest_zero, 1)
                max_turn(0, 0)
                scores_max(0, 1, 0, NSM)
                pe.wait_ge(ones_ready, RING)
                scores(0, 0, 0, 0)
                scores(0, 0, 0, 1)

                def body(i, s, left):
                    for kt in range(KT):
                        n = kt * SM_KT
                        ahead = [(i, s, kt + 1)] if kt + 1 < KT else [(i, s + 1, 0)] if left >= 1 else []
                        for pair in range(2):
                            if ahead:
                                scores(*ahead[0], pair)
                            if left >= 2:
                                scores_max(i, s + 2, n + pair * SM_KT // 4, n + (pair + 1) * SM_KT // 4)
                        for half in range(2):
                            values(i, s, kt, half)
                            if left >= 2:
                                scores_max(i, s + 2, n + (half + 2) * SM_KT // 4, n + (half + 3) * SM_KT // 4)
                        if kt == 2 and left >= 1:
                            max_turn(i, s + 1)
                bodies(pe, body)

            @block.scalar
            def _(act):
                def copy_out(i, s):
                    n = (s - 1) % 2
                    act.wait_ge(o_out[n], i * (16 * RING // 2) + (16 * ((s - 1) // 2) + 32))
                    act.wait_ge(pv_done, i * (RING * KT) + (s * KT + 2))
                    act.copy(OE[n][:, :], pO[n][:, :]).then_inc(o_sb, 1)

                act.sem_inc(p_sb, 2)
                act.wait_ge(o_sb, 1)

                def body(i, s, left):
                    for kt in range(KT):
                        act.wait_ge(pv_done, i * (RING * KT) + (s * KT + kt + 1))
                        for pair in range(2):
                            act.wait_ge(s_ps, i * (RING * 2 * KT) + (s * 2 * KT + kt * 2 + pair + 1))
                            act.activation(PR[2 * (kt % 2) + pair][:, :, :], pS[pair][:, :, :], ACT.Exp,
                                           scale=HD ** -0.5).then_inc(p_sb, 1)
                        if kt == 0:
                            copy_out(i, s)
                bodies(act, body)
                copy_out(NI // RING - 1, RING)

            @block.vector
            def _(dve):
                chain = Chain(dve, mchain_s)
                chain.step(dve.memset(pO[0][:, :], 0.0))
                dve.memset(pO[1][:, :], 0.0).then_inc(o_sb, 1)
                dve.wait_ge(id_ready, 2)
                dve.tensor_copy(identb[:, :], ident[:, :]).then_inc(id_ready, 1)
                dve.memset(MS[:, 3:, :], 0.0).then_inc(rest_zero, 1)
                dve.memset(ZERO[:, :], 0.0).then_inc(zeroed, 1)
                dve.sem_inc(x_max, 2)

                def maxima(i, s, n0, n1):
                    for n in range(n0, n1):
                        dve.wait_ge(x_ps, i * (RING * NSM) + (s * NSM + n + 1))
                        dve.tensor_reduce(MX[:, n:n + 1], pX[n % 2][:, :], AX.X, ALU.max
                                          ).then_inc(x_max, 1)

                def split(i, s):
                    chain.at(i * (RING * 4) + (s * 4 + 1))
                    dve.wait_ge(x_max, i * (RING * NSM) + ((s + 1) * NSM + 2))
                    chain.step(dve.tensor_reduce(MN[:, :], MX[:, :].rearrange("p (x a) -> p x a", a=QC),
                                                 AX.X, ALU.max, negate=True))
                    chain.step(dve.tensor_copy(MS[:, 0, :], MN[:, :]))
                    chain.step(dve.tensor_tensor(MR[:, :], MN[:, :], MS[:, 0, :], ALU.subtract))
                    chain.step(dve.tensor_copy(MS[:, 1, :], MR[:, :]))
                    dve.tensor_tensor(MS[:, 2, :], MR[:, :], MS[:, 1, :], ALU.subtract).then_inc(m_split, 1)

                def turned(i, s):
                    dve.wait_ge(m_ps, i * RING + (s + 1))
                    dve.tensor_copy(MB[s % 2][:, :], turned_max(s)).then_inc(m_sb, 1)

                maxima(0, 0, 0, NSM)
                split(0, 0)
                turned(0, 0)
                maxima(0, 1, 0, NSM)

                def body(i, s, left):
                    if left >= 1:
                        split(i, s + 1)
                    if left >= 2:
                        maxima(i, s + 2, 0, 3 * SM_KT)
                    if left >= 1:
                        turned(i, s + 1)
                    if left >= 2:
                        maxima(i, s + 2, 3 * SM_KT, NSM)
                bodies(dve, body)


def phase_mamba(nc, xnT_d, w_in, conv_w, conv_b, w_x, w_dt, b_dt, a_log, d_skip, w_out, bc_d, mo_d, batches):
    C, T = xnT_d.shape
    DI = w_out.shape[0]
    N = a_log.shape[1] // (DI // P)
    R = w_dt.shape[0]
    KC, JT = C // P, DI // P
    NCH = T // BANK
    CB = NCH // batches
    QN = 4
    NQ = N // QN
    TG = BANK // P
    TAPS = conv_w.shape[1] // JT
    NPS = 2 * JT + 1 + JT
    assert NCH % 2 == 0 and CB % 2 == 0 and NQ == 4 and JT == 4
    with ExitStack() as ctx:
        m = Place(nc, ctx, "mamba")
        WIN = m.sb("win", [P, KC, 2 * DI])
        WX = m.sb("wx", [P, JT, R + 2 * N])
        WDT = m.sb("wdt", [R, DI])
        WOUT = m.sb("wout", [P, JT, C])
        CW = m.sb("cw", [P, JT, TAPS])
        CBI = m.sb("cb", [P, JT])
        BDT = m.sb("bdt", [P, JT])
        AN = m.sb("an", [P, JT, N])
        DS = m.sb("ds", [P, JT])
        MK = m.sb("mk", [P, NCH])
        ident = m.sb("ident", [P, P])
        HS = m.sb("hs", [P, JT, N])
        CR = m.sb("cr", [P, JT, TAPS - 1])
        XT = [m.sb(f"xt{s}", [P, KC, BANK]) for s in range(2)]
        XC = m.sb("xc", [P, JT, BANK + TAPS - 1])
        XV = m.sb("xv", [P, JT, BANK])
        XS = [m.sb(f"xs{s}", [P, JT, BANK]) for s in range(2)]
        GT = [m.sb(f"gt{s}", [P, JT, BANK]) for s in range(2)]
        DT = [m.sb(f"dt{s}", [P, JT, BANK]) for s in range(2)]
        U = [m.sb(f"u{s}", [P, JT, BANK]) for s in range(2)]
        DR = m.sb("dr", [R + 2 * N, BANK])
        BQ = [m.sb(f"bq{n}", [P, 2, QN, BANK]) for n in range(2)]
        DA = [m.sb(f"da{n}", [P, QN, BANK]) for n in range(2)]
        DB = [m.sb(f"db{n}", [P, QN, BANK]) for n in range(2)]
        H = [m.sb(f"h{n}", [P, QN, BANK]) for n in range(2)]
        Z = m.sb("z", [P, JT, BANK])
        MO = m.sb("mo", [P, TG, C])
        E = XC[:, :, TAPS - 1:TAPS - 1 + BANK]
        pY = [m.ps(f"pY{j}", [P, BANK]) for j in range(JT)]
        pP = [m.ps(f"pP{n}", [P, BANK]) for n in range(2)]
        pW = [m.ps(f"pW{n}", [P, BANK]) for n in range(2)]
        w_ld = m.sem("w_ld")
        id_ready = m.sem("id_ready")
        ready = m.sem("ready")
        a_ready = m.sem("a_ready")
        xt_in = [m.sem(f"xt_in{s}") for s in range(2)]
        p_ps = m.sem("p_ps")
        p_sb = m.sem("p_sb")
        steps_s = m.sem("steps")
        conv_done = m.sem("conv_done")
        cr_kept = m.sem("cr_kept")
        xc_free = m.sem("xc_free")
        xs_done = m.sem("xs_done")
        bc_out = m.sem("bc_out")
        bc_there = m.sem("bc_there")
        b_in = [m.sem(f"b_in{n}") for n in range(2)]
        c_in = [m.sem(f"c_in{n}") for n in range(2)]
        e_done = m.sem("e_done")
        dt_part = m.sem("dt_part")
        dt_done = m.sem("dt_done")
        u_done = m.sem("u_done")
        da_done = m.sem("da_done")
        db_done = m.sem("db_done")
        scanned = m.sem("scanned")
        hs_kept = m.sem("hs_kept")
        hc_done = m.sem("hc_done")
        y_done = m.sem("y_done")
        z_raw = m.sem("z_raw")
        z_done = m.sem("z_done")
        w_ps = m.sem("w_ps")
        w_sb = m.sem("w_sb")
        mo_out = m.sem("mo_out")
        UNITS = NQ * JT

        def bodies(eng, body):
            body(0, 0, 0, True, NCH == 1, NCH > 2)
            looped = max(0, (NCH - 3) // 2)
            if looped:
                with eng.Fori(0, looped) as i:
                    body(i * 2 + 1, i, 1, False, False, True)
                    body(i * 2 + 2, i + 1, 0, False, False, True)
            for c in range(1 + 2 * looped, NCH):
                body(c, c // 2, c % 2, False, c == NCH - 1, c + 2 < NCH)

        with nc.Block() as block:

            @block.sync
            def _(sp):
                for dst, src in ((WIN[:, :, :], w_in.rearrange("(k p) n -> p k n", p=P)),
                                 (WX[:, :, :], w_x.rearrange("(k p) n -> p k n", p=P)),
                                 (WDT[:, :], w_dt),
                                 (WOUT[:, :, :], w_out.rearrange("(k p) n -> p k n", p=P)),
                                 (CW[:, :, :], conv_w.rearrange("p (j k) -> p j k", j=JT)),
                                 (CBI[:, :], conv_b), (BDT[:, :], b_dt),
                                 (AN[:, :, :], a_log.rearrange("p (j n) -> p j n", j=JT)), (DS[:, :], d_skip)):
                    sp.dma_start(dst, src).then_inc(w_ld, 16)

                def load_x(c, s):
                    sp.dma_start(XT[s][:, :, :],
                                 xnT_d[:, ds(c * BANK, BANK)].rearrange("(k p) t -> p k t", p=P)
                                 ).then_inc(xt_in[s], 16)

                def load_rows(c, q, n, done):
                    rows = bc_d[ds(c, 1), n * N + q * QN:n * N + (q + 1) * QN, :]
                    sp.dma_start(BQ[q % 2][:, n, :, :],
                                 rows.rearrange("c n t -> c (n t)").to_broadcast([P, QN * BANK])
                                 ).then_inc(done[q % 2], 16)

                def load_b(c, q):
                    if q == 0:
                        sp.wait_ge(bc_out, c * 16 + 16)
                        sp.sem_inc(bc_there, 1)
                    sp.wait_ge(db_done, c * UNITS + (q * JT + JT))
                    load_rows(c, q, 0, b_in)

                def load_c(c, q):
                    sp.wait_ge(hc_done, c * UNITS + (q * JT + JT))
                    load_rows(c, q, 1, c_in)

                def store_mo(c):
                    sp.wait_ge(w_sb, c * 2 + 4)
                    sp.dma_start(mo_d[ds(c * BANK, BANK), :].rearrange("(t p) c -> p t c", p=P),
                                 MO[:, :, :]).then_inc(mo_out, 16)

                def store_bc(c):
                    sp.wait_ge(p_sb, c * NPS + (JT + 3))
                    sp.dma_start(bc_d[ds(c, 1), :, :].rearrange("c n t -> (c n) t"), DR[R:R + 2 * N, :]
                                 ).then_inc(bc_out, 16)

                load_x(0, 0)
                load_x(1, 1)
                store_bc(0)
                load_b(0, 0)
                load_c(0, 0)
                load_b(0, 1)

                def body(c, u, s, first, last, more):
                    if more:
                        sp.wait_ge(p_ps, c * NPS + NPS)
                        load_x(c + 2, s)
                    load_c(c, 1)
                    load_b(c, 2)
                    load_c(c, 2)
                    if not first:
                        store_mo(c - 1)
                    load_b(c, 3)
                    load_c(c, 3)
                    if not last:
                        store_bc(c + 1)
                        load_b(c + 1, 0)
                        load_c(c + 1, 0)
                        load_b(c + 1, 1)
                    else:
                        store_mo(c)
                bodies(sp, body)
                sp.wait_ge(mo_out, 16 * NCH + 16)

            @block.gpsimd
            def _(pool):
                pool.sem_inc(db_done, 8)
                make_identity(pool, ident, id_ready)

                def softplus(c, s, part):
                    if part == 0:
                        pool.wait_ge(e_done, c * 5 + 5)
                        pool.wait_ge(xc_free, c + 2)
                        pool.tensor_tensor(DT[s][:, :, :], DT[s][:, :, :], U[s][:, :, :], ALU.subtract
                                           ).then_inc(dt_part, 1)
                    else:
                        pool.wait_ge(dt_part, c + 1)
                        pool.tensor_tensor(DT[s][:, :, :], DT[s][:, :, :], XV[:, :, :], ALU.add
                                           ).then_inc(dt_done, 1)

                def u_step(c, s):
                    pool.wait_ge(dt_done, c + 1)
                    pool.tensor_tensor(U[s][:, :, :], DT[s][:, :, :], XS[s][:, :, :], ALU.mult
                                       ).then_inc(u_done, 1)
                    pool.wait_ge(u_done, c + 1)

                softplus(0, 0, 0)
                softplus(0, 0, 1)
                u_step(0, 0)

                def body(c, u, s, first, last, more):
                    for k in range(UNITS):
                        q, j = divmod(k, JT)
                        if j == 0:
                            pool.wait_ge(b_in[q % 2], c * 32 + (16 * (q // 2) + 16))
                        pool.wait_ge(scanned, c * UNITS + (k + 1))
                        pool.tensor_tensor(DB[k % 2][:, :, :], BQ[q % 2][:, 0, :, :],
                                           U[s][:, j, :].unsqueeze(1).to_broadcast([P, QN, BANK]), ALU.mult
                                           ).then_inc(db_done, 1)
                        if k == 12 and not last:
                            softplus(c + 1, 1 - s, 0)
                        if k == 13 and not last:
                            softplus(c + 1, 1 - s, 1)
                        if k == 14 and not last:
                            u_step(c + 1, 1 - s)
                bodies(pool, body)

            @block.scalar
            def _(act):
                act.wait_ge(w_ld, 16 * 9)
                act.activation(AN[:, :, :], AN[:, :, :], ACT.Exp).then_inc(a_ready, 1)

                def bank(s, n):
                    return pP[(s + n) % 2]

                def conv_in(c, s, tiles=range(JT)):
                    act.wait_ge(xc_free, c + 1)
                    for j in tiles:
                        act.wait_ge(p_ps, c * NPS + (j + 1))
                        act.copy(XC[:, j, TAPS - 1:], bank(s, j)[:, :])
                        act.activation(XV[:, j, :], bank(s, j)[:, :], ACT.Identity,
                                       scale=CW[:, j, TAPS - 1:], bias=CBI[:, j:j + 1]).then_inc(p_sb, 1)

                def conv_out(c, s):
                    for j in range(JT):
                        act.wait_ge(conv_done, c * JT + (j + 1))
                        act.activation(XS[s][:, j, :], XV[:, j, :], ACT.Silu).then_inc(xs_done, 1)
                def gate_out(c, s, tiles=range(JT)):
                    for j in tiles:
                        n = 2 * JT + 1 + j
                        act.wait_ge(p_ps, c * NPS + (n + 1))
                        act.activation(GT[s][:, j, :], bank(s, n)[:, :], ACT.Silu).then_inc(p_sb, 1)

                def low_rank(c, s, first=False):
                    act.wait_ge(p_ps, c * NPS + (JT + 1))
                    if not first:
                        act.wait_ge(bc_out, c * 16)
                    act.copy(DR[:, :], bank(s, JT)[0:R + 2 * N, :]).then_inc(p_sb, 1)

                def dt_raw(c, s, tiles=range(JT)):
                    for j in tiles:
                        n = JT + 1 + j
                        act.wait_ge(p_ps, c * NPS + (n + 1))
                        act.activation(XV[:, j, :], bank(s, n)[:, :], ACT.Identity, bias=BDT[:, j:j + 1]
                                       ).then_inc(p_sb, 1)

                def soft_in(c, s):
                    act.wait_ge(p_sb, c * NPS + (2 * JT + 3))
                    act.wait_ge(cr_kept, c + 1)
                    act.activation(E, XV[:, :, :], ACT.Abs).then_inc(e_done, 1)
                    act.wait_ge(e_done, c * 5 + 1)
                    act.activation(E, E, ACT.Exp, scale=-1.0).then_inc(e_done, 1)
                    act.wait_ge(e_done, c * 5 + 2)
                    act.activation(U[s][:, :, :], E, ACT.Identity, bias=1.0).then_inc(e_done, 1)
                    act.activation(XV[:, :, :], XV[:, :, :], ACT.Relu).then_inc(e_done, 1)
                    act.activation(DT[s][:, :, :], E, ACT.Ln, bias=1.0).then_inc(e_done, 1)

                def decay(c, s, k):
                    q, j = divmod(k, JT)
                    act.wait_ge(scanned, c * UNITS + (k + 1))
                    for n in range(QN):
                        ins = act.activation(DA[k % 2][:, n, :], DT[s][:, j, :], ACT.Exp,
                                             scale=AN[:, j, q * QN + n:q * QN + n + 1])
                    ins.then_inc(da_done, 1)

                def mo_copy(c):
                    act.wait_ge(mo_out, c * 16 + 16)
                    for n in range(2):
                        act.wait_ge(w_ps, c * 2 + (n + 3))
                        act.copy(MO[:, 2 * n:2 * n + 2, :], pW[n][:, :]).then_inc(w_sb, 1)

                act.sem_inc(p_sb, 2)
                act.sem_inc(w_sb, 2)
                act.sem_inc(mo_out, 16)
                act.wait_ge(ready, 1)
                conv_in(0, 0)
                conv_out(0, 0)
                low_rank(0, 0, first=True)
                dt_raw(0, 0)
                soft_in(0, 0)
                gate_out(0, 0)

                def body(c, u, s, first, last, more):
                    act.wait_ge(dt_done, c + 1)
                    for k in range(UNITS):
                        decay(c, s, k)
                        if k == 4 and not first:
                            mo_copy(c - 1)
                        if not last:
                            if k == 1:
                                conv_in(c + 1, 1 - s, (0, 1))
                            if k == 3:
                                conv_in(c + 1, 1 - s, (2, 3))
                            if k == 5:
                                conv_out(c + 1, 1 - s)
                            if k == 7:
                                low_rank(c + 1, 1 - s)
                            if k == 9:
                                dt_raw(c + 1, 1 - s, (0, 1))
                            if k == 11:
                                dt_raw(c + 1, 1 - s, (2, 3))
                                soft_in(c + 1, 1 - s)
                            if k == 13:
                                gate_out(c + 1, 1 - s, (0, 1))
                            if k == 15:
                                gate_out(c + 1, 1 - s, (2, 3))
                    if last:
                        mo_copy(c)
                bodies(act, body)

            @block.tensor
            def _(pe):
                def into(c, s, n, pairs, rows=P):
                    pe.wait_ge(p_sb, c * NPS + (n + 1))
                    for i, (w, x) in enumerate(pairs):
                        mm = pe.matmul(pP[(s + n) % 2][0:rows, :], w, x, start=(i == 0),
                                       stop=(i == len(pairs) - 1))
                    mm.then_inc(p_ps, 1)

                def project_in(c, u, s, half, tiles=range(JT)):
                    pe.wait_ge(xt_in[s], u * 16 + 16)
                    for j in tiles:
                        w = slice((half * JT + j) * P, (half * JT + j + 1) * P)
                        into(c, s, half * (2 * JT + 1) + j, [(WIN[:, k, w], XT[s][:, k, :]) for k in range(KC)])

                def low_rank(c, s):
                    pe.wait_ge(xs_done, c * JT + JT)
                    into(c, s, JT, [(WX[:, j, :], XS[s][:, j, :]) for j in range(JT)], R + 2 * N)

                def dt_in(c, s, tiles=range(JT)):
                    pe.wait_ge(p_sb, c * NPS + (JT + 3))
                    for j in tiles:
                        into(c, s, JT + 1 + j, [(WDT[:, j * P:(j + 1) * P], DR[0:R, :])])

                def project_out(c):
                    pe.wait_ge(z_done, c * JT + JT)
                    for n in range(2):
                        pe.wait_ge(w_sb, c * 2 + (n + 1))
                        for t in range(2):
                            for j in range(JT):
                                mm = pe.matmul(pW[n][:, t * C:(t + 1) * C],
                                               Z[:, j, (2 * n + t) * P:(2 * n + t + 1) * P],
                                               WOUT[:, j, :], start=(j == 0), stop=(j == JT - 1))
                        mm.then_inc(w_ps, 1)

                pe.sem_inc(y_done, 2)
                pe.sem_inc(w_ps, 2)
                pe.wait_ge(w_ld, 16 * 9)
                pe.wait_ge(id_ready, 2)
                project_in(0, 0, 0, 0)
                low_rank(0, 0)
                dt_in(0, 0)
                project_in(0, 0, 0, 1)

                def body(c, u, s, first, last, more):
                    if not last:
                        project_in(c + 1, u + s, 1 - s, 0, (0, 1))
                    for k in range(UNITS):
                        q, j = divmod(k, JT)
                        if q == 0:
                            pe.wait_ge(z_raw, c * JT + (j + 1))
                        pe.wait_ge(hc_done, c * UNITS + (k + 9))
                        for n in range(QN):
                            mm = pe.matmul(pY[j][:, :], ident[:, :], H[k % 2][:, n, :],
                                           start=(q == 0 and n == 0), stop=(q == NQ - 1 and n == QN - 1))
                        mm.then_inc(y_done, 1)
                        if k == 1 and not first:
                            project_out(c - 1)
                        if not last:
                            if k == 0:
                                project_in(c + 1, u + s, 1 - s, 0, (2, 3))
                            if k == 4:
                                low_rank(c + 1, 1 - s)
                            if k == 6:
                                dt_in(c + 1, 1 - s, (0, 1))
                            if k == 8:
                                dt_in(c + 1, 1 - s, (2, 3))
                            if k == 10:
                                project_in(c + 1, u + s, 1 - s, 1, (0, 1))
                            if k == 12:
                                project_in(c + 1, u + s, 1 - s, 1, (2, 3))
                    if last:
                        project_out(c)
                bodies(pe, body)

            @block.vector
            def _(dve):
                def conv(c, s, chain):
                    dve.wait_ge(p_sb, c * NPS + (JT + 2))
                    chain.step(dve.tensor_scalar(XC[:, :, 0:TAPS - 1], CR[:, :, :], MK[:, ds(c, 1)],
                                                 None, ALU.mult))
                    for k in range(TAPS - 1):
                        for j in range(JT):
                            ins = dve.scalar_tensor_tensor(out=XV[:, j, :], in0=XC[:, j, k:k + BANK],
                                                           scalar=CW[:, j, k:k + 1], in1=XV[:, j, :],
                                                           op0=ALU.mult, op1=ALU.add)
                            if k == TAPS - 2:
                                ins.then_inc(conv_done, 1)
                        if k < TAPS - 2:
                            chain.step(ins)
                    dve.wait_ge(conv_done, c * JT + JT)
                    dve.tensor_copy(CR[:, :, :], XC[:, :, BANK:BANK + TAPS - 1]).then_inc(cr_kept, 1)
                    dve.wait_ge(cr_kept, c + 1)

                def lost(c, s):
                    dve.wait_ge(e_done, c * 5 + 3)
                    dve.scalar_tensor_tensor(out=U[s][:, :, :], in0=U[s][:, :, :], scalar=1.0, in1=E,
                                             op0=ALU.subtract, op1=ALU.subtract).then_inc(xc_free, 1)

                def gated(c, s, j):
                    if j == 0:
                        dve.wait_ge(w_ps, c * 2 + 2)
                    dve.wait_ge(y_done, c * UNITS + (UNITS - JT + j + 3))
                    dve.scalar_tensor_tensor(out=Z[:, j, :], in0=XS[s][:, j, :], scalar=DS[:, j:j + 1],
                                             in1=pY[j][:, :], op0=ALU.mult, op1=ALU.add
                                             ).then_inc(z_raw, 1)
                    dve.wait_ge(z_raw, c * JT + (JT + j + 1))
                    dve.tensor_tensor(Z[:, j, :], Z[:, j, :], GT[s][:, j, :], ALU.mult
                                      ).then_inc(z_done, 1)

                chain = Chain(dve, steps_s)
                dve.sem_inc(xc_free, 1)
                dve.sem_inc(scanned, 2)
                dve.sem_inc(hc_done, 8)
                dve.sem_inc(z_raw, JT)
                chain.step(dve.memset(MK[:, :], 1.0))
                for b in range(batches):
                    chain.step(dve.memset(MK[:, b * CB:b * CB + 1], 0.0))
                chain.step(dve.memset(HS[:, :, :], 0.0))
                chain.step(dve.memset(CR[:, :, :], 0.0))
                dve.wait_ge(w_ld, 16 * 9)
                dve.wait_ge(a_ready, 1)
                dve.tensor_scalar(AN[:, :, :], AN[:, :, :], -1.0, None, ALU.mult).then_inc(ready, 1)
                made = chain.n
                chain.at(made)
                conv(0, 0, chain)
                lost(0, 0)
                PER = chain.n

                def body(c, u, s, first, last, more):
                    dve.tensor_scalar(HS[:, :, :], HS[:, :, :], MK[:, ds(c, 1)], None, ALU.mult
                                      ).then_inc(hs_kept, 1)
                    dve.wait_ge(hs_kept, c * (UNITS + 1) + 1)
                    chain.at(c * PER + (made + PER))
                    for k in range(UNITS):
                        q, j = divmod(k, JT)
                        h = H[k % 2]
                        dve.wait_ge(da_done, c * UNITS + (k + 1))
                        dve.wait_ge(db_done, c * UNITS + (k + 9))
                        dve.wait_ge(y_done, c * UNITS + (k + 1))
                        for n in range(QN):
                            ins = dve.tensor_tensor_scan(h[:, n, :], DA[k % 2][:, n, :], DB[k % 2][:, n, :],
                                                         HS[:, j, q * QN + n:q * QN + n + 1],
                                                         ALU.mult, ALU.add)
                        ins.then_inc(scanned, 1)
                        dve.wait_ge(scanned, c * UNITS + (k + 3))
                        dve.tensor_copy(HS[:, j, q * QN:(q + 1) * QN], h[:, :, BANK - 1]
                                        ).then_inc(hs_kept, 1)
                        dve.wait_ge(hs_kept, c * (UNITS + 1) + (k + 2))
                        if j == 0:
                            dve.wait_ge(c_in[q % 2], c * 32 + (16 * (q // 2) + 16))
                        dve.tensor_tensor(h[:, :, :], h[:, :, :], BQ[q % 2][:, 1, :, :], ALU.mult
                                          ).then_inc(hc_done, 1)
                        if not last and k == 2:
                            conv(c + 1, 1 - s, chain)
                        if k == 0 and not first:
                            gated(c - 1, 1 - s, JT - 1)
                        if k > UNITS - JT:
                            gated(c, s, k - (UNITS - JT + 1))
                        if not last and k == 11:
                            lost(c + 1, 1 - s)
                    if last:
                        gated(c, s, JT - 1)
                bodies(dve, body)


def phase_route(nc, x, xn_d, mo_d, oraw_d, wo, bo, g2, b2, gate_w, gate_b, slots_d, BASE, SLOT, TE, batches):
    T, C = x.shape
    NT, KC, TG = T // P, C // P, BANK // P
    NB = T // batches // BANK
    NE = gate_w.shape[1]
    NTL = TE.shape[1]
    GB = HEADS // GH
    QC = NB
    RING = min(4, NB)
    assert NB % RING == 0
    with ExitStack() as ctx:
        m = Place(nc, ctx, "route")
        WO = m.sb("wo", [P, KC, C])
        BO = m.sb("bo", [1, C])
        GW = m.sb("gw", [P, KC, NE])
        GBI = m.sb("gb", [1, NE])
        G = m.sb("g", [P, C])
        B = m.sb("b", [P, C])
        ONE = m.sb("one", [1, P])
        ident = m.sb("ident", [P, P])
        LOWER = m.sb("lower", [P, P])
        ALL = m.sb("all", [P, P])
        OT = [m.sb(f"ot{s}", [P, KC, BANK]) for s in range(RING)]
        SM = [m.sb(f"sm{s}", [P, KC, BANK]) for s in range(RING)]
        XN = [m.sb(f"xn{s}", [P, TG, C]) for s in range(RING)]
        XR = [m.sb(f"xr{s}", [P, 2, TG, C]) for s in range(RING)]
        X1 = m.sb("x1", [P, NT, C])
        HN = m.sb("hn", [P, NT, C])
        ST = m.sb("stats", [P, TG, 6])
        MV = m.sb("meanvar", [P, TG, 2])
        V, ROOT, RS, TMP = (m.sb(n, [P, TG]) for n in ("var", "root", "rstd", "tmp"))
        HT = [m.sb(f"ht{n}", [P, 2, KC, P]) for n in range(2)]
        LG, EQ, OH, TOT, INC, POS = (m.sb(n, [P, NT, NE]) for n in ("lg", "eq", "oh", "tot", "inc", "pos"))
        WT = m.sb("wt", [P, NE])
        MXL = m.sb("mxl", [P, NT])
        MW = m.sb("mw", [P, NT])
        CNT, NBF, BEND, BST = (m.sb(n, [P, NE]) for n in ("cnt", "nbf", "bend", "bst"))
        CNTI = m.sb("cnti", [P, NE], I32)
        UNIT = m.sb("unit", [P, max(NT, NE)])
        JT = m.sb("jt", [P, NTL])
        CMP = m.sb("cmp", [P, NTL, NE])
        TEF = m.sb("tef", [P, NTL])
        pA = [m.ps(f"pA{n}", [P, C]) for n in range(TG)]
        pT = [m.ps(f"pT{n}", [P, 2, KC, P]) for n in range(2)]
        pG = m.ps("pG", [P, NT, NE])
        pCN = m.ps("pCN", [P, 2, NT, NE])
        w_in = m.sem("w_in")
        id_ready = m.sem("id_ready")
        consts = m.sem("consts")
        o_in = [m.sem(f"o_in{s}") for s in range(RING)]
        scale_s = m.sem("scale")
        a_ps = m.sem("a_ps")
        x1_done = m.sem("x1_done")
        x1_read = m.sem("x1_read")
        norm_s = m.sem("norm")
        waited_v = m.sem("waited_v")
        waited_p = m.sem("waited_p")
        base_s = m.sem("base")
        chain_s = m.sem("chain")
        var_ready = m.sem("var_ready")
        root_ready = m.sem("root_ready")
        hn_raw = m.sem("hn_raw")
        hn_mul = m.sem("hn_mul")
        hn_done = m.sem("hn_done")
        t_ps = m.sem("t_ps")
        t_sb = m.sem("t_sb")
        g_ps = m.sem("g_ps")
        oh_done = m.sem("oh_done")
        n_ps = m.sem("n_ps")
        slot_done = m.sem("slot_done")
        sent = m.sem("sent")

        NCH = batches * NB

        def use(b, cb):
            return b * NB + cb, b * (NB // RING) + cb // RING

        def chunks(eng, body):
            def batch(b, last):
                for cb in range(NB):
                    c, u = use(b, cb)
                    body(b, cb, c, u, cb % RING, last and cb == NB - 1)
            if batches > 1:
                with eng.Fori(0, batches - 1) as b:
                    batch(b, False)
            batch(batches - 1, True)

        with nc.Block() as block:

            @block.sync
            def _(sp):
                for dst, src in ((WO[:, :, :], wo.rearrange("(k p) n -> p k n", p=P)),
                                 (BO[:, :], bo.rearrange("(o n) -> o n", o=1)),
                                 (GW[:, :, :], gate_w.rearrange("(k p) n -> p k n", p=P)),
                                 (GBI[:, :], gate_b.rearrange("(o n) -> o n", o=1)),
                                 (G[:, :], bcast_rows(g2, P)), (B[:, :], bcast_rows(b2, P))):
                    sp.dma_start(dst, src).then_inc(w_in, 16)

                def body(b, cb, c, u, s, last):
                    sp.wait_ge(base_s, c * 2 + 2)
                    for k in range(KC):
                        for g in range(2):
                            raw = oraw_d[ds(b * (GB * QC) + (2 * k + g) * QC + cb, 1), :, :] \
                                .rearrange("i (h r) q -> h (i r) q", r=P // GH)
                            half = slice(g * GH * HD, (g + 1) * GH * HD)
                            sp.dma_start(OT[s][half, k, :], raw[:, 0:HD, :]).then_inc(o_in[s], 16)
                            sp.dma_start(SM[s][half, k, :],
                                         raw[:, HD:VW, :].to_broadcast([GH, HD, BANK])).then_inc(o_in[s], 16)
                    rows = ds(c * BANK, BANK)
                    sp.dma_start(XN[s][:, :, :], xn_d[rows, :].rearrange("(t p) c -> p t c", p=P)
                                 ).then_inc(o_in[s], 16)
                    for n, src in enumerate((x, mo_d)):
                        sp.dma_start(XR[s][:, n, :, :], src[rows, :].rearrange("(t p) c -> p t c", p=P)
                                     ).then_inc(o_in[s], 16)
                chunks(sp, body)

            @block.gpsimd
            def _(pool):
                make_identity(pool, ident, id_ready)
                pool.iota(JT[:, :], pattern=[[1, NTL]], base=0, channel_multiplier=0,
                          allow_small_or_imprecise_dtypes=True).then_inc(consts, 1)
                pool.iota(WT[:, :], pattern=[[-1, NE]], base=NE, channel_multiplier=0,
                          allow_small_or_imprecise_dtypes=True).then_inc(consts, 1)
                pool.wait_ge(consts, 5)
                pool.affine_select(out=LOWER[:, :], in_=ALL[:, :], compare_op=ALU.is_gt, fill=0.0, base=0,
                                   pattern=[[1, P]], channel_multiplier=-1).then_inc(consts, 1)
                pool.sem_inc(base_s, 2 * RING)

                def body(b, cb, c, u, s, last):
                    pool.wait_ge(o_in[s], u * 176 + 176)
                    pool.tensor_tensor(XR[s][:, 0, :, :], XR[s][:, 0, :, :], XR[s][:, 1, :, :], ALU.add
                                       ).then_inc(base_s, 1)
                    pool.wait_ge(base_s, c * 2 + (2 * RING + 1))
                    pool.wait_ge(x1_done, c * TG + TG)
                    pool.tensor_tensor(BASE[:, ds(c * TG, TG), :], XR[s][:, 0, :, :],
                                       X1[:, ds(c * TG, TG), :], ALU.add).then_inc(base_s, 1)
                    h = HN[:, ds(c * TG, TG), :]
                    pool.wait_ge(hn_raw, c + 1)
                    pool.tensor_tensor(h, h, G[:, :].unsqueeze(1).to_broadcast([P, TG, C]), ALU.mult
                                       ).then_inc(hn_mul, 1)
                    pool.wait_ge(hn_mul, c + 1)
                    pool.sem_inc(waited_p, 1)
                    pool.tensor_tensor(h, h, B[:, :].unsqueeze(1).to_broadcast([P, TG, C]), ALU.add
                                       ).then_inc(hn_done, 1)
                chunks(pool, body)
                pool.wait_ge(slot_done, 1)
                for t in range(NT):
                    pool.indirect_dma_start(out=slots_d, out_offset=bass.IndirectOffsetOnAxis(
                        ap=SLOT[:, t:t + 1], axis=0), in_=HN[:, t, :], in_offset=None).then_inc(sent, 16)
                pool.wait_ge(sent, 16 * NT)

            @block.tensor
            def _(pe):
                pe.wait_ge(w_in, 16 * 6)
                pe.wait_ge(id_ready, 2)
                pe.wait_ge(consts, 6)

                def body(b, cb, c, u, s, last):
                    pe.wait_ge(scale_s, c * 2 + 2)
                    for t in range(TG):
                        pe.wait_ge(x1_read, c * TG + (t + 1))
                        for k in range(KC):
                            pe.matmul(pA[t][:, :], OT[s][:, k, t * P:(t + 1) * P], WO[:, k, :],
                                      start=(k == 0), stop=False)
                        pe.matmul(pA[t][:, :], ONE[:, :], BO[:, :], start=False, stop=True
                                  ).then_inc(a_ps, 1)
                chunks(pe, body)

                def gate(n):
                    pe.wait_ge(t_sb, n + 1)
                    for h in range(2):
                        t = 2 * n + h
                        for k in range(KC):
                            pe.matmul(pG[:, t, :], HT[n % 2][:, h, k, :], GW[:, k, :], start=(k == 0),
                                      stop=False)
                        mm = pe.matmul(pG[:, t, :], ONE[:, :], GBI[:, :], start=False, stop=True)
                    mm.then_inc(g_ps, 1)

                for n in range(NT // 2):
                    pe.wait_ge(hn_done, 2 * n // TG + 1)
                    if n >= 2:
                        pe.wait_ge(t_sb, n - 1)
                    for h in range(2):
                        for k in range(KC):
                            mm = pe.transpose(pT[n % 2][:, h, k, :], HN[:, 2 * n + h, k * P:(k + 1) * P],
                                              ident[:, :])
                    mm.then_inc(t_ps, 1)
                    if n >= 1:
                        gate(n - 1)
                gate(NT // 2 - 1)
                pe.wait_ge(oh_done, 1)
                pe.matmul(pCN[:, 0, :, :], LOWER[:, :], OH[:, :, :], start=True, stop=True).then_inc(n_ps, 1)
                pe.matmul(pCN[:, 1, :, :], ALL[:, :], OH[:, :, :], start=True, stop=True).then_inc(n_ps, 1)

            @block.scalar
            def _(act):
                with act.Fori(0, NCH) as c:
                    act.wait_ge(var_ready, c + 1)
                    act.activation(ROOT[:, :], V[:, :], ACT.Sqrt).then_inc(root_ready, 1)
                for n in range(NT // 2):
                    act.wait_ge(t_ps, n + 1)
                    if n >= 2:
                        act.wait_ge(g_ps, n - 1)
                    act.copy(HT[n % 2][:, :, :, :], pT[n % 2][:, :, :, :]).then_inc(t_sb, 1)

            @block.vector
            def _(dve):
                chain = Chain(dve, chain_s)
                dve.memset(ONE[:, :], 1.0).then_inc(consts, 1)
                dve.memset(ALL[:, :], 1.0).then_inc(consts, 1)
                dve.memset(UNIT[:, :], 1.0).then_inc(consts, 1)
                dve.sem_inc(x1_read, TG)
                dve.wait_ge(w_in, 16 * 6)
                norm = Chain(dve, norm_s)

                def scale(c, u, s):
                    dve.wait_ge(o_in[s], u * 176 + 176)
                    dve.reciprocal(SM[s][:, :, :], SM[s][:, :, :]).then_inc(scale_s, 1)
                    dve.wait_ge(scale_s, c * 2 + 1)
                    dve.tensor_tensor(OT[s][:, :, :], OT[s][:, :, :], SM[s][:, :, :], ALU.mult
                                      ).then_inc(scale_s, 1)

                scale(0, 0, 0)
                PER = TG + 5

                def body(b, cb, c, u, s, last):
                    if not last:
                        scale(*use(b, cb + 1), (cb + 1) % RING)
                    norm.at(c * PER)
                    for t in range(TG):
                        row = X1[:, ds(c * TG + t, 1), :]
                        dve.wait_ge(a_ps, c * TG + (t + 1))
                        dve.tensor_tensor(row, pA[t][:, :].unsqueeze(1), XN[s][:, t:t + 1, :], ALU.add
                                          ).then_inc(x1_done, 1)
                        dve.wait_ge(x1_done, c * TG + (t + 1))
                        dve.sem_inc(waited_v, 1)
                        dve.bn_stats(ST[:, t:t + 1, :], row).then_inc(x1_read, 1)
                    dve.wait_ge(x1_read, c * TG + 2 * TG)
                    dve.sem_inc(waited_v, 1)
                    for t in range(TG):
                        norm.mark(dve.bn_aggr(MV[:, t, :], ST[:, t, :]))
                    norm.join()
                    dve.tensor_scalar(V[:, :], MV[:, :, 1], EPS, None, ALU.add).then_inc(var_ready, 1)
                    rstd_steps(dve, norm, V[:, :], ROOT[:, :], RS[:, :], TMP[:, :], var_ready, root_ready,
                               c + 1)
                    assert norm.n == PER
                    for t in range(TG):
                        ins = dve.tensor_scalar(HN[:, ds(c * TG + t, 1), :], X1[:, ds(c * TG + t, 1), :],
                                                MV[:, t, 0:1], RS[:, t:t + 1], ALU.subtract, ALU.mult)
                    ins.then_inc(hn_raw, 1)
                chunks(dve, body)

                def over_e(ap):
                    return ap.unsqueeze(2).to_broadcast([P, NT, NE])

                def over_t(ap):
                    return ap.unsqueeze(1).to_broadcast([P, NT, NE])

                dve.wait_ge(consts, 6)
                dve.wait_ge(g_ps, NT // 2)
                chain.step(dve.tensor_copy(LG[:, :, :], pG[:, :, :]))
                chain.step(dve.tensor_reduce(MXL[:, :], LG[:, :, :], AX.X, ALU.max))
                chain.step(dve.tensor_tensor(EQ[:, :, :], LG[:, :, :], over_e(MXL[:, :]), ALU.is_equal))
                chain.step(dve.tensor_tensor(EQ[:, :, :], EQ[:, :, :], over_t(WT[:, :]), ALU.mult))
                chain.step(dve.tensor_reduce(MW[:, :], EQ[:, :, :], AX.X, ALU.max))
                chain.step(dve.tensor_copy(EQ[:, :, :], over_t(WT[:, :])))
                dve.tensor_tensor(OH[:, :, :], EQ[:, :, :], over_e(MW[:, :]), ALU.is_equal
                                  ).then_inc(oh_done, 1)
                dve.wait_ge(n_ps, 2)
                dve.wait_ge(oh_done, 1)
                chain.step(dve.tensor_copy(TOT[:, :, :], pCN[:, 1, :, :]))
                for e in range(NE):
                    ins = dve.tensor_tensor_scan(INC[:, :, e], UNIT[:, 0:NT], TOT[:, :, e], 0.0,
                                                 ALU.mult, ALU.add)
                chain.step(ins)
                chain.step(dve.tensor_tensor(POS[:, :, :], INC[:, :, :], TOT[:, :, :], ALU.subtract))
                chain.step(dve.tensor_tensor(POS[:, :, :], POS[:, :, :], pCN[:, 0, :, :], ALU.add))
                chain.step(dve.tensor_scalar(CNT[:, :], INC[:, NT - 1, :], float(MT - 1), None, ALU.add))
                chain.step(dve.tensor_copy(CNTI[:, :], CNT[:, :]))
                chain.step(dve.tensor_scalar(CNTI[:, :], CNTI[:, :], MT.bit_length() - 1, None,
                                             ALU.logical_shift_right))
                chain.step(dve.tensor_copy(NBF[:, :], CNTI[:, :]))
                chain.step(dve.tensor_tensor_scan(BEND[:, :], UNIT[:, 0:NE], NBF[:, :], 0.0, ALU.mult, ALU.add))
                chain.step(dve.tensor_tensor(BST[:, :], BEND[:, :], NBF[:, :], ALU.subtract))
                chain.step(dve.scalar_tensor_tensor(out=POS[:, :, :], in0=over_t(BST[:, :]), scalar=float(MT),
                                                    in1=POS[:, :, :], op0=ALU.mult, op1=ALU.add))
                chain.step(dve.tensor_tensor(POS[:, :, :], POS[:, :, :], OH[:, :, :], ALU.mult))
                chain.step(dve.tensor_reduce(MW[:, :], POS[:, :, :], AX.X, ALU.add))
                dve.tensor_copy(SLOT[:, :], MW[:, :]).then_inc(slot_done, 1)
                shape = [P, NTL, NE]
                chain.step(dve.tensor_tensor(CMP[:, :, :], JT[:, :].unsqueeze(2).to_broadcast(shape),
                                             BEND[:, :].unsqueeze(1).to_broadcast(shape), ALU.is_ge))
                chain.step(dve.tensor_reduce(TEF[:, :], CMP[:, :, :], AX.X, ALU.add))
                chain.step(dve.tensor_scalar(TEF[:, :], TEF[:, :], float(NE - 1), None, ALU.min))
                chain.step(dve.tensor_copy(TE[:, :], TEF[:, :]))


def phase_experts(nc, w1, b1, w2, b2, slots_d, ys_d, TE):
    E, C, F = w1.shape
    NTL = TE.shape[1]
    KC, KF, TT = C // P, F // P, MT // P
    with ExitStack() as ctx:
        m = Place(nc, ctx, "exp")
        W1 = [m.sb(f"w1{s}", [P, KC, F]) for s in range(2)]
        W2 = [m.sb(f"w2{s}", [P, KF, C]) for s in range(2)]
        B1 = [m.sb(f"b1{s}", [P, KF]) for s in range(2)]
        B2 = [m.sb(f"b2{s}", [1, C]) for s in range(2)]
        XR = [m.sb(f"xr{s}", [P, TT, C]) for s in range(2)]
        XT = [m.sb(f"xt{s}", [P, KC, MT]) for s in range(2)]
        HM = [m.sb(f"hm{s}", [P, KF, MT]) for s in range(2)]
        YO = [m.sb(f"yo{s}", [P, TT, C]) for s in range(2)]
        ONE = m.sb("one", [1, P])
        ident = m.sb("ident", [P, P])
        pT = [m.ps(f"pT{n}", [P, KC, MT]) for n in range(2)]
        pH = [m.ps(f"pH{n}", [P, 2, MT]) for n in range(KF // 2)]
        pY = [m.ps(f"pY{n}", [P, TT, C]) for n in range(2)]
        id_ready = m.sem("id_ready")
        one_ready = m.sem("one_ready")
        x_in = [m.sem(f"x_in{s}") for s in range(2)]
        w1_in = [m.sem(f"w1_in{s}") for s in range(2)]
        w2_in = [m.sem(f"w2_in{s}") for s in range(2)]
        x_ps = m.sem("x_ps")
        x_sb = m.sem("x_sb")
        h_ps = m.sem("h_ps")
        h_act = m.sem("h_act")
        h_dve = m.sem("h_dve")
        y_ps = m.sem("y_ps")
        y_sb = m.sem("y_sb")
        y_out = [m.sem(f"y_out{s}") for s in range(2)]
        NH = KF // 2

        def bodies(eng, body):
            pairs = (NTL - 1) // 2
            with eng.Fori(0, pairs) as i:
                for s in range(2):
                    body(i * 2 + s, i, s, False)
            for j in range(2 * pairs, NTL):
                body(j, j // 2, j % 2, j == NTL - 1)

        with nc.Block() as block:

            @block.sync
            def _(sp):
                def load(j, s):
                    e = sp.value_load(TE[0:1, ds(j, 1)], min_val=0, max_val=E - 1)
                    sp.dma_start(XR[s][:, :, :],
                                 slots_d[ds(j * MT, MT), :].rearrange("(t p) c -> p t c", p=P)
                                 ).then_inc(x_in[s], 16)
                    sp.dma_start(W1[s][:, :, :], w1[ds(e, 1), :, :].rearrange("e (k p) f -> p (e k) f", p=P)
                                 ).then_inc(w1_in[s], 16)
                    sp.dma_start(B1[s][:, :], b1[ds(e, 1), :, :].rearrange("e p k -> (e p) k")
                                 ).then_inc(w1_in[s], 16)
                    sp.dma_start(W2[s][:, :, :], w2[ds(e, 1), :, :].rearrange("e (k p) c -> p (e k) c", p=P)
                                 ).then_inc(w2_in[s], 16)
                    sp.dma_start(B2[s][:, :], b2[ds(e, 1), :]).then_inc(w2_in[s], 16)

                for s in range(2):
                    sp.sem_inc(y_out[s], 16)
                load(0, 0)

                def body(j, u, s, last):
                    if not last:
                        sp.wait_ge(y_ps, j + 2)
                        sp.wait_ge(h_act, j * (NH // 2) + NH // 2)
                        sp.wait_ge(h_dve, j * (NH // 2) + NH // 2)
                        load(j + 1, 1 - s)
                    sp.wait_ge(y_sb, j + 3)
                    sp.dma_start(ys_d[ds(j * MT, MT), :].rearrange("(t p) c -> p t c", p=P),
                                 YO[s][:, :, :]).then_inc(y_out[s], 16)
                bodies(sp, body)
                sp.wait_ge(y_out[0], 16 * ((NTL + 1) // 2 + 1))
                sp.wait_ge(y_out[1], 16 * (NTL // 2 + 1))

            @block.gpsimd
            def _(pool):
                make_identity(pool, ident, id_ready)

            @block.tensor
            def _(pe):
                def turn(j, u, s):
                    pe.wait_ge(x_in[s], u * 16 + 16)
                    pe.wait_ge(x_sb, j + 1)
                    for k in range(KC):
                        for t in range(TT):
                            mm = pe.transpose(pT[s][:, k, t * P:(t + 1) * P],
                                              XR[s][:, t, k * P:(k + 1) * P], ident[:, :])
                    mm.then_inc(x_ps, 1)

                pe.sem_inc(y_ps, 2)
                pe.wait_ge(id_ready, 2)
                pe.wait_ge(one_ready, 1)
                turn(0, 0, 0)

                def body(j, u, s, last):
                    pe.wait_ge(x_sb, j + 3)
                    pe.wait_ge(w1_in[s], u * 32 + 32)
                    for n in range(NH):
                        pe.wait_ge((h_act, h_dve)[n % 2], j * (NH // 2) + (n // 2 + 1))
                        for f in range(2 * n, 2 * n + 2):
                            for k in range(KC):
                                mm = pe.matmul(pH[n][:, f % 2, :], W1[s][:, k, f * P:(f + 1) * P],
                                               XT[s][:, k, :], start=(k == 0), stop=(k == KC - 1))
                        mm.then_inc(h_ps, 1)
                    if not last:
                        turn(j + 1, u + s, 1 - s)
                    pe.wait_ge(w2_in[s], u * 32 + 32)
                    pe.wait_ge(y_sb, j + 1)
                    for t in range(TT):
                        for f in range(KF):
                            if t == 0 and f % 2 == 0:
                                n = f // 2
                                pe.wait_ge((h_act, h_dve)[n % 2], j * (NH // 2) + (NH // 2 + n // 2 + 1))
                            pe.matmul(pY[s][:, t, :], HM[s][:, f, t * P:(t + 1) * P], W2[s][:, f, :],
                                      start=(f == 0), stop=False)
                        mm = pe.matmul(pY[s][:, t, :], ONE[:, :], B2[s][:, :], start=False, stop=True)
                    mm.then_inc(y_ps, 1)
                bodies(pe, body)

            @block.scalar
            def _(act):
                act.sem_inc(h_act, NH // 2)
                act.sem_inc(y_sb, 2)

                def body(j, u, s, last):
                    act.wait_ge(w1_in[s], u * 32 + 32)
                    for n in range(0, NH, 2):
                        act.wait_ge(h_ps, j * NH + (n + 1))
                        act.activation(HM[s][:, 2 * n, :], pH[n][:, 0, :], ACT.Relu,
                                       bias=B1[s][:, 2 * n:2 * n + 1])
                        act.activation(HM[s][:, 2 * n + 1, :], pH[n][:, 1, :], ACT.Relu,
                                       bias=B1[s][:, 2 * n + 1:2 * n + 2]).then_inc(h_act, 1)
                    act.wait_ge(y_ps, j + 3)
                    act.wait_ge(y_out[s], u * 16 + 16)
                    act.copy(YO[s][:, :, :], pY[s][:, :, :]).then_inc(y_sb, 1)
                bodies(act, body)

            @block.vector
            def _(dve):
                dve.memset(ONE[:, :], 1.0).then_inc(one_ready, 1)
                dve.sem_inc(x_sb, 2)
                dve.sem_inc(h_dve, NH // 2)

                def turned(j, s):
                    dve.wait_ge(x_ps, j + 1)
                    dve.tensor_copy(XT[s][:, :, :], pT[s][:, :, :]).then_inc(x_sb, 1)

                turned(0, 0)

                def body(j, u, s, last):
                    dve.wait_ge(w1_in[s], u * 32 + 32)
                    for n in range(1, NH, 2):
                        dve.wait_ge(h_ps, j * NH + (n + 1))
                        dve.tensor_scalar(HM[s][:, 2 * n, :], pH[n][:, 0, :], B1[s][:, 2 * n:2 * n + 1], 0.0,
                                          ALU.add, ALU.max)
                        dve.tensor_scalar(HM[s][:, 2 * n + 1, :], pH[n][:, 1, :],
                                          B1[s][:, 2 * n + 1:2 * n + 2], 0.0, ALU.add, ALU.max
                                          ).then_inc(h_dve, 1)
                    if not last:
                        turned(j + 1, 1 - s)
                bodies(dve, body)


def phase_output(nc, ys_d, out, BASE, SLOT):
    T, C = out.shape
    NT, TG = T // P, BANK // P
    with ExitStack() as ctx:
        m = Place(nc, ctx, "out")
        Y = m.sb("y", [P, NT, C])
        got = [m.sem(f"got{g}") for g in range(NT // TG)]
        added = m.sem("added")
        stored = m.sem("stored")

        with nc.Block() as block:

            @block.gpsimd
            def _(pool):
                for t in range(NT):
                    pool.indirect_dma_start(out=Y[:, t, :], out_offset=None, in_=ys_d,
                                            in_offset=bass.IndirectOffsetOnAxis(ap=SLOT[:, t:t + 1], axis=0)
                                            ).then_inc(got[t // TG], 16)

            @block.vector
            def _(dve):
                for g in range(NT // TG):
                    rows = slice(g * TG, (g + 1) * TG)
                    dve.wait_ge(got[g], 16 * TG)
                    dve.tensor_tensor(Y[:, rows, :], Y[:, rows, :], BASE[:, rows, :], ALU.add).then_inc(added, 1)

            @block.sync
            def _(sp):
                for g in range(NT // TG):
                    sp.wait_ge(added, g + 1)
                    sp.dma_start(out[g * BANK:(g + 1) * BANK, :].rearrange("(t p) c -> p t c", p=P),
                                 Y[:, g * TG:(g + 1) * TG, :]).then_inc(stored, 16)
                sp.wait_ge(stored, 16 * (NT // TG))


def build(nc, a, out, batches):
    x = a["x"]
    T, C = x.shape
    L = T // batches
    NCH = T // BANK
    E = a["w1"].shape[0]
    N2 = a["w_x"].shape[1] - a["w_dt"].shape[0]
    NTL = T // MT + E - 1

    def scratch(name, shape, dt=F32):
        return nc.dram_tensor(name, shape, dt).ap()

    xn_d = scratch("xn_d", [T, C])
    xnT_d = scratch("xnT_d", [C, T])
    parts_d = scratch("parts_d", [2, 3, batches * C, L], BF16)
    v_d = scratch("v_d", [batches * HEADS // GH, L, GH * VW])
    bc_d = scratch("bc_d", [NCH, N2, BANK])
    mo_d = scratch("mo_d", [T, C])
    oraw_d = scratch("oraw_d", [batches * HEADS // GH * (L // BANK), P, BANK])
    slots_d = scratch("slots_d", [NTL * MT, C])
    ys_d = scratch("ys_d", [NTL * MT, C])

    phase_project(nc, x, a["ln1_g"], a["ln1_b"], a["wq"], a["bq"], a["wk"], a["bk"], a["wv"], a["bv"],
                  xn_d, xnT_d, parts_d, v_d, batches)
    phase_mamba(nc, xnT_d, a["w_in"], a["conv_w"], a["conv_b"], a["w_x"], a["w_dt"], a["b_dt"],
                a["a_log"], a["d_skip"], a["w_out"], bc_d, mo_d, batches)
    phase_attention(nc, parts_d, v_d, oraw_d, slots_d, batches)
    with ExitStack() as ctx:
        m = Place(nc, ctx, "kept")
        BASE = m.sb("base", [P, T // P, C])
        SLOT = m.sb("slot", [P, T // P], I32)
        TE = m.sb("te", [P, NTL], I32)
        phase_route(nc, x, xn_d, mo_d, oraw_d, a["wo"], a["bo"], a["ln2_g"], a["ln2_b"],
                    a["gate_w"], a["gate_b"], slots_d, BASE, SLOT, TE, batches)
        phase_experts(nc, a["w1"], a["b1"], a["w2"], a["b2"], slots_d, ys_d, TE)
        phase_output(nc, ys_d, out, BASE, SLOT)


def lay_out(inputs):
    import numpy as np

    def whole(a):
        return np.ascontiguousarray(a)

    def tiles(a):
        a = np.asarray(a)
        a = a.reshape(a.shape[0] // P, P, -1)
        return whole(a.transpose(1, 0, 2).reshape(P, -1))

    t = {k: np.asarray(v) for k, v in inputs.items()}
    x = t["L0_attn_x"]
    mamba = {n: t[f"L0_attn_{k}"] for n, k in (("w_in", "W_in"), ("w_x", "W_x"), ("w_dt", "W_dt"),
                                               ("w_out", "W_out"))}
    mamba |= {n: tiles(t[f"L0_attn_{k}"]) for n, k in (("conv_w", "conv_w"), ("conv_b", "conv_b"),
                                                       ("b_dt", "b_dt"), ("a_log", "A_log"), ("d_skip", "D"))}
    ffn = {n: t[f"L0_ffn_{n}"] for n in ("ln1_g", "ln1_b", "ln2_g", "ln2_b", "wq", "wk", "wv", "bv", "wo",
                                         "bo", "gate_w", "gate_b", "w1", "w2", "b2")}
    ffn |= {n: tiles(t[f"L0_ffn_{n}"]) for n in ("bq", "bk")}
    b1 = t["L0_ffn_b1"]
    ffn["b1"] = whole(b1.reshape(b1.shape[0], -1, P).transpose(0, 2, 1))
    return {"x": whole(x.reshape(-1, x.shape[-1]))} | {k: whole(v) for k, v in (mamba | ffn).items()}


def kernel(**inputs):
    import concourse.bacc as bacc
    from concourse.bass_utils import run_bass_kernel_spmd

    shape = inputs["L0_attn_x"].shape
    arrays = lay_out(inputs)
    nc = bacc.Bacc("TRN2", target_bir_lowering=False, num_devices=1)
    args = {n: nc.dram_tensor(f"in_{n}", v.shape, mybir.dt.from_np(v.dtype), kind="ExternalInput").ap()
            for n, v in arrays.items()}
    out = nc.dram_tensor("out_0", list(arrays["x"].shape), F32, kind="ExternalOutput").ap()
    build(nc, args, out, shape[0])
    r = run_bass_kernel_spmd(nc, [{f"in_{n}": v for n, v in arrays.items()}], core_ids=[0])
    return r.results[0]["out_0"].reshape(shape)
```
